# Optimizing a Trainium2 kernel written in Bass

```python
import numpy as np
import jax
import jax.numpy as jnp

def _softmax(x, axis=-1):
    return jax.nn.softmax(x, axis=axis)

def _gelu(x):
    return jax.nn.gelu(x, approximate=True)

def _silu(x):
    return jax.nn.silu(x)

def _sigmoid(x):
    return jax.nn.sigmoid(x)

def _layernorm(x, axis=-1, eps=1e-05):
    m = jnp.mean(x, axis=axis, keepdims=True)
    v = jnp.var(x, axis=axis, keepdims=True)
    return (x - m) / jnp.sqrt(v + eps)

def _scatter_add(tgt, idx, src, axis=0):
    return tgt.at[idx].add(src)

def _segment_sum(src, seg, n):
    return jax.ops.segment_sum(src, seg, n)
kernel_name = 'mk_cond_seq_d2_seqx_r8_16196d'

def setup_inputs(seed: int=0):
    np.random.seed(seed)
    _w = jnp.asarray

    def _rec_inputs():
        import jax
        import jax.numpy as jnp
        _rk = jax.random.key(seed)
        x = -0.0002928 + 1 * jax.random.normal(jax.random.fold_in(_rk, 1), (4, 256, 128), jnp.float32)
        _lenS = 256 - jax.random.randint(jax.random.fold_in(_rk, 7), (4,), 0, max(1, 256 // 4) + 1, jnp.int32)
        _lenS2 = 256 - jax.random.randint(jax.random.fold_in(_rk, 8), (4,), 0, max(1, 256 // 4) + 1, jnp.int32)
        cond_1024 = 0.0061147 + 1.02565 * jax.random.normal(jax.random.fold_in(_rk, 11), (4, 128), jnp.float32)
        return (x, cond_1024)
    x, cond_1024 = _rec_inputs()

    def _L0_cond_setup():
        import jax, jax.numpy as jnp
        import numpy as np
        D = 128
        H = 16
        HD = 4 * D
        B, T = (4, 128)
        EPS = 1e-05

        def _layernorm(x, g, b):
            mu = jnp.mean(x, axis=-1, keepdims=True)
            var = jnp.mean(jnp.square(x - mu), axis=-1, keepdims=True)
            return (x - mu) * jax.lax.rsqrt(var + EPS) * g + b

        def _attention(x, Wqkv, Wproj, bproj):
            b, t, c = x.shape
            hd = c // H
            qkv = (x @ Wqkv).reshape(b, t, 3, H, hd).transpose(2, 0, 3, 1, 4)
            q, k, v = (qkv[0], qkv[1], qkv[2])
            scale = hd ** (-0.5)
            scores = jnp.einsum('bhqd,bhkd->bhqk', q, k) * scale
            causal = jnp.tril(jnp.ones((t, t), bool))
            scores = jnp.where(causal, scores, -jnp.inf)
            attn = jax.nn.softmax(scores, axis=-1)
            out = jnp.einsum('bhqk,bhkd->bhqd', attn, v)
            out = out.transpose(0, 2, 1, 3).reshape(b, t, c)
            return out @ Wproj + bproj
        key = jax.random.key(seed)
        ks = jax.random.split(key, 12)
        s = 0.02
        return {'x': jax.random.normal(ks[0], (B, T, D), jnp.float32), 'condition': jax.random.normal(ks[1], (B, D), jnp.float32), 'Wqkv': jax.random.normal(ks[2], (D, 3 * D), jnp.float32) * s, 'Wproj': jax.random.normal(ks[3], (D, D), jnp.float32) * s, 'bproj': jnp.zeros((D,), jnp.float32), 'W1': jax.random.normal(ks[4], (D, HD), jnp.float32) * s, 'b1': jnp.zeros((HD,), jnp.float32), 'W2': jax.random.normal(ks[5], (HD, D), jnp.float32) * s, 'b2': jnp.zeros((D,), jnp.float32), 'g1': jnp.ones((D,), jnp.float32), 'be1': jnp.zeros((D,), jnp.float32), 'g2': jnp.ones((D,), jnp.float32), 'be2': jnp.zeros((D,), jnp.float32), 'Wada': jax.random.normal(ks[6], (D, 6 * D), jnp.float32) * s, 'bada': jax.random.normal(ks[7], (6 * D,), jnp.float32) * s}
    _L0_cond_all = _L0_cond_setup()
    _L0_cond_in = {k: v for k, v in _L0_cond_all.items() if k in ('Wqkv', 'Wproj', 'bproj', 'W1', 'b1', 'W2', 'b2', 'g1', 'be1', 'g2', 'be2', 'Wada', 'bada')}
    del _L0_cond_all

    def _L1_cond_setup():
        import jax, jax.numpy as jnp
        import numpy as np
        D_MODEL = 128
        N_HEADS = 16
        HEAD_DIM = D_MODEL // N_HEADS
        D_FF = 512
        EPS = 1e-05
        THETA = 10000.0
        B, S = (2, 256)

        def _rope_cache(seq_len, head_dim, theta=THETA):
            inv_freq = 1.0 / theta ** (jnp.arange(0, head_dim, 2, dtype=jnp.float32) / head_dim)
            t = jnp.arange(seq_len, dtype=jnp.float32)
            freqs = jnp.einsum('i,j->ij', t, inv_freq)
            emb = jnp.concatenate([freqs, freqs], axis=-1)
            return (jnp.cos(emb), jnp.sin(emb))

        def _rotate_half(x):
            x1, x2 = jnp.split(x, 2, axis=-1)
            return jnp.concatenate([-x2, x1], axis=-1)

        def _ada_rmsnorm(x, time_emb, weight, w1, b1, w2, b2):
            h = jax.nn.silu(time_emb @ w1 + b1)
            scale, shift = jnp.split(h @ w2 + b2, 2, axis=-1)
            norm = x * jax.lax.rsqrt(jnp.mean(x * x, axis=-1, keepdims=True) + EPS)
            return norm * weight * (1.0 + scale[:, None, :]) + shift[:, None, :]
        key = jax.random.key(seed)
        ks = jax.random.split(key, 24)
        rn = lambda k, shp: jax.random.normal(k, shp, dtype=jnp.float32) * 0.02
        return {'x': jax.random.normal(ks[0], (B, S, D_MODEL), dtype=jnp.float32), 'time_emb': jax.random.normal(ks[1], (B, D_MODEL), dtype=jnp.float32), 'w_norm1': jnp.ones((D_MODEL,), jnp.float32), 't1_w1': rn(ks[2], (D_MODEL, D_MODEL)), 't1_b1': jnp.zeros((D_MODEL,), jnp.float32), 't1_w2': rn(ks[3], (D_MODEL, 2 * D_MODEL)), 't1_b2': jnp.zeros((2 * D_MODEL,), jnp.float32), 'w_norm2': jnp.ones((D_MODEL,), jnp.float32), 't2_w1': rn(ks[4], (D_MODEL, D_MODEL)), 't2_b1': jnp.zeros((D_MODEL,), jnp.float32), 't2_w2': rn(ks[5], (D_MODEL, 2 * D_MODEL)), 't2_b2': jnp.zeros((2 * D_MODEL,), jnp.float32), 'wq': rn(ks[6], (D_MODEL, D_MODEL)), 'bq': jnp.zeros((D_MODEL,), jnp.float32), 'wk': rn(ks[7], (D_MODEL, D_MODEL)), 'bk': jnp.zeros((D_MODEL,), jnp.float32), 'wv': rn(ks[8], (D_MODEL, D_MODEL)), 'bv': jnp.zeros((D_MODEL,), jnp.float32), 'wo': rn(ks[9], (D_MODEL, D_MODEL)), 'bo': jnp.zeros((D_MODEL,), jnp.float32), 'w_gate': rn(ks[10], (D_MODEL, D_FF)), 'w_up': rn(ks[11], (D_MODEL, D_FF)), 'w_down': rn(ks[12], (D_FF, D_MODEL))}
    _L1_cond_all = _L1_cond_setup()
    _L1_cond_in = {k: v for k, v in _L1_cond_all.items() if k in ('w_norm1', 't1_w1', 't1_b1', 't1_w2', 't1_b2', 'w_norm2', 't2_w1', 't2_b1', 't2_w2', 't2_b2', 'wq', 'bq', 'wk', 'bk', 'wv', 'bv', 'wo', 'bo', 'w_gate', 'w_up', 'w_down')}
    del _L1_cond_all
    return {'x': x, 'cond_1024': cond_1024, 'L0_cond_Wqkv': _L0_cond_in['Wqkv'], 'L0_cond_Wproj': _L0_cond_in['Wproj'], 'L0_cond_bproj': _L0_cond_in['bproj'], 'L0_cond_W1': _L0_cond_in['W1'], 'L0_cond_b1': _L0_cond_in['b1'], 'L0_cond_W2': _L0_cond_in['W2'], 'L0_cond_b2': _L0_cond_in['b2'], 'L0_cond_g1': _L0_cond_in['g1'], 'L0_cond_be1': _L0_cond_in['be1'], 'L0_cond_g2': _L0_cond_in['g2'], 'L0_cond_be2': _L0_cond_in['be2'], 'L0_cond_Wada': _L0_cond_in['Wada'], 'L0_cond_bada': _L0_cond_in['bada'], 'L1_cond_w_norm1': _L1_cond_in['w_norm1'], 'L1_cond_t1_w1': _L1_cond_in['t1_w1'], 'L1_cond_t1_b1': _L1_cond_in['t1_b1'], 'L1_cond_t1_w2': _L1_cond_in['t1_w2'], 'L1_cond_t1_b2': _L1_cond_in['t1_b2'], 'L1_cond_w_norm2': _L1_cond_in['w_norm2'], 'L1_cond_t2_w1': _L1_cond_in['t2_w1'], 'L1_cond_t2_b1': _L1_cond_in['t2_b1'], 'L1_cond_t2_w2': _L1_cond_in['t2_w2'], 'L1_cond_t2_b2': _L1_cond_in['t2_b2'], 'L1_cond_wq': _L1_cond_in['wq'], 'L1_cond_bq': _L1_cond_in['bq'], 'L1_cond_wk': _L1_cond_in['wk'], 'L1_cond_bk': _L1_cond_in['bk'], 'L1_cond_wv': _L1_cond_in['wv'], 'L1_cond_bv': _L1_cond_in['bv'], 'L1_cond_wo': _L1_cond_in['wo'], 'L1_cond_bo': _L1_cond_in['bo'], 'L1_cond_w_gate': _L1_cond_in['w_gate'], 'L1_cond_w_up': _L1_cond_in['w_up'], 'L1_cond_w_down': _L1_cond_in['w_down']}

def reference(x, cond_1024, L0_cond_Wqkv, L0_cond_Wproj, L0_cond_bproj, L0_cond_W1, L0_cond_b1, L0_cond_W2, L0_cond_b2, L0_cond_g1, L0_cond_be1, L0_cond_g2, L0_cond_be2, L0_cond_Wada, L0_cond_bada, L1_cond_w_norm1, L1_cond_t1_w1, L1_cond_t1_b1, L1_cond_t1_w2, L1_cond_t1_b2, L1_cond_w_norm2, L1_cond_t2_w1, L1_cond_t2_b1, L1_cond_t2_w2, L1_cond_t2_b2, L1_cond_wq, L1_cond_bq, L1_cond_wk, L1_cond_bk, L1_cond_wv, L1_cond_bv, L1_cond_wo, L1_cond_bo, L1_cond_w_gate, L1_cond_w_up, L1_cond_w_down):
    import jax
    import jax.numpy as jnp

    def _L0_cond_ref(x, condition, Wqkv, Wproj, bproj, W1, b1, W2, b2, g1, be1, g2, be2, Wada, bada):
        import jax, jax.numpy as jnp
        import numpy as np
        D = 128
        H = 16
        HD = 4 * D
        B, T = (4, 128)
        EPS = 1e-05

        def _layernorm(x, g, b):
            mu = jnp.mean(x, axis=-1, keepdims=True)
            var = jnp.mean(jnp.square(x - mu), axis=-1, keepdims=True)
            return (x - mu) * jax.lax.rsqrt(var + EPS) * g + b

        def _attention(x, Wqkv, Wproj, bproj):
            b, t, c = x.shape
            hd = c // H
            qkv = (x @ Wqkv).reshape(b, t, 3, H, hd).transpose(2, 0, 3, 1, 4)
            q, k, v = (qkv[0], qkv[1], qkv[2])
            scale = hd ** (-0.5)
            scores = jnp.einsum('bhqd,bhkd->bhqk', q, k) * scale
            causal = jnp.tril(jnp.ones((t, t), bool))
            scores = jnp.where(causal, scores, -jnp.inf)
            attn = jax.nn.softmax(scores, axis=-1)
            out = jnp.einsum('bhqk,bhkd->bhqd', attn, v)
            out = out.transpose(0, 2, 1, 3).reshape(b, t, c)
            return out @ Wproj + bproj
        mod = jax.nn.silu(condition) @ Wada + bada
        sh_a, sc_a, gt_a, sh_m, sc_m, gt_m = jnp.split(mod, 6, axis=1)
        xn = _layernorm(x, g1, be1)
        xm = xn * (1.0 + sc_a[:, None, :]) + sh_a[:, None, :]
        x = x + gt_a[:, None, :] * _attention(xm, Wqkv, Wproj, bproj)
        xn = _layernorm(x, g2, be2)
        xm = xn * (1.0 + sc_m[:, None, :]) + sh_m[:, None, :]
        h = jax.nn.gelu(xm @ W1 + b1, approximate=False)
        x = x + gt_m[:, None, :] * (h @ W2 + b2)
        return x

    def _L1_cond_ref(x, time_emb, w_norm1, t1_w1, t1_b1, t1_w2, t1_b2, w_norm2, t2_w1, t2_b1, t2_w2, t2_b2, wq, bq, wk, bk, wv, bv, wo, bo, w_gate, w_up, w_down):
        import jax, jax.numpy as jnp
        import numpy as np
        D_MODEL = 128
        N_HEADS = 16
        HEAD_DIM = D_MODEL // N_HEADS
        D_FF = 512
        EPS = 1e-05
        THETA = 10000.0
        B, S = (2, 256)

        def _rope_cache(seq_len, head_dim, theta=THETA):
            inv_freq = 1.0 / theta ** (jnp.arange(0, head_dim, 2, dtype=jnp.float32) / head_dim)
            t = jnp.arange(seq_len, dtype=jnp.float32)
            freqs = jnp.einsum('i,j->ij', t, inv_freq)
            emb = jnp.concatenate([freqs, freqs], axis=-1)
            return (jnp.cos(emb), jnp.sin(emb))

        def _rotate_half(x):
            x1, x2 = jnp.split(x, 2, axis=-1)
            return jnp.concatenate([-x2, x1], axis=-1)

        def _ada_rmsnorm(x, time_emb, weight, w1, b1, w2, b2):
            h = jax.nn.silu(time_emb @ w1 + b1)
            scale, shift = jnp.split(h @ w2 + b2, 2, axis=-1)
            norm = x * jax.lax.rsqrt(jnp.mean(x * x, axis=-1, keepdims=True) + EPS)
            return norm * weight * (1.0 + scale[:, None, :]) + shift[:, None, :]
        b, s, _ = x.shape
        cos, sin = _rope_cache(s, HEAD_DIM)
        nx = _ada_rmsnorm(x, time_emb, w_norm1, t1_w1, t1_b1, t1_w2, t1_b2)
        q = (nx @ wq + bq).reshape(b, s, N_HEADS, HEAD_DIM)
        k = (nx @ wk + bk).reshape(b, s, N_HEADS, HEAD_DIM)
        v = (nx @ wv + bv).reshape(b, s, N_HEADS, HEAD_DIM)
        c = cos[:, None, :]
        si = sin[:, None, :]
        q = q * c + _rotate_half(q) * si
        k = k * c + _rotate_half(k) * si
        scores = jnp.einsum('bshd,bthd->bhst', q, k) / jnp.sqrt(jnp.float32(HEAD_DIM))
        probs = jax.nn.softmax(scores, axis=-1)
        attn = jnp.einsum('bhst,bthd->bshd', probs, v).reshape(b, s, D_MODEL)
        x = x + attn @ wo + bo
        nx = _ada_rmsnorm(x, time_emb, w_norm2, t2_w1, t2_b1, t2_w2, t2_b2)
        gate = jax.nn.gelu(nx @ w_gate, approximate=False)
        ff = gate * (nx @ w_up) @ w_down
        return x + ff
    x = _L0_cond_ref(x, cond_1024, L0_cond_Wqkv, L0_cond_Wproj, L0_cond_bproj, L0_cond_W1, L0_cond_b1, L0_cond_W2, L0_cond_b2, L0_cond_g1, L0_cond_be1, L0_cond_g2, L0_cond_be2, L0_cond_Wada, L0_cond_bada)
    x = _L1_cond_ref(x, cond_1024, L1_cond_w_norm1, L1_cond_t1_w1, L1_cond_t1_b1, L1_cond_t1_w2, L1_cond_t1_b2, L1_cond_w_norm2, L1_cond_t2_w1, L1_cond_t2_b1, L1_cond_t2_w2, L1_cond_t2_b2, L1_cond_wq, L1_cond_bq, L1_cond_wk, L1_cond_bk, L1_cond_wv, L1_cond_bv, L1_cond_wo, L1_cond_bo, L1_cond_w_gate, L1_cond_w_up, L1_cond_w_down)
    return x

_drawn_inputs = setup_inputs


def setup_inputs(seed=0):
    import zlib

    import numpy as np

    out = dict(_drawn_inputs(seed))
    spreads = {'L0_cond_bproj': (0.0, 0.644),
     'L0_cond_b1': (0.0, 0.8),
     'L0_cond_b2': (0.0, 0.57),
     'L0_cond_g1': (1.0, 0.6),
     'L0_cond_be1': (0.0, 0.8),
     'L0_cond_g2': (1.0, 0.6),
     'L0_cond_be2': (0.0, 0.8),
     'L1_cond_w_norm1': (1.0, 0.6),
     'L1_cond_t1_b1': (0.0, 0.8),
     'L1_cond_t1_b2': (0.0, 0.8),
     'L1_cond_w_norm2': (1.0, 0.6),
     'L1_cond_t2_b1': (0.0, 0.8),
     'L1_cond_t2_b2': (0.0, 0.8),
     'L1_cond_bq': (0.0, 0.8),
     'L1_cond_bk': (0.0, 0.8),
     'L1_cond_bv': (0.0, 2.0),
     'L1_cond_bo': (0.0, 0.532)}
    factors = {'cond_1024': 2.93,
     'L0_cond_Wqkv': 8.0,
     'L0_cond_Wproj': 8.0,
     'L0_cond_W1': 6.993,
     'L0_cond_W2': 6.259,
     'L0_cond_bada': 8.0,
     'L1_cond_t1_w1': 8.0,
     'L1_cond_t1_w2': 8.0,
     'L1_cond_t2_w1': 8.0,
     'L1_cond_t2_w2': 8.0,
     'L1_cond_wq': 8.0,
     'L1_cond_wk': 8.0,
     'L1_cond_wv': 8.0,
     'L1_cond_w_gate': 3.944,
     'L1_cond_w_up': 3.921,
     'L1_cond_w_down': 3.93}
    for name, (base, spread) in spreads.items():
        noise = np.random.default_rng([zlib.crc32(name.encode()), seed]).standard_normal(out[name].shape)
        drawn = base * np.exp(spread * noise) if base else spread * noise
        out[name] = jnp.asarray(drawn.astype(out[name].dtype))
    for name, factor in factors.items():
        out[name] = (out[name] * factor).astype(out[name].dtype)
    return out
```

```python
from contextlib import ExitStack

import numpy as np

import concourse.bass as bass
from concourse import mybir

ALU = mybir.AluOpType
ACT = mybir.ActivationFunctionType
F32 = mybir.dt.float32
BF16 = mybir.dt.bfloat16
AX_X = mybir.AxisListType.X

P = 128
B, T, D = 4, 256, 128
H, HD = 16, 8
NT = T // P
LAYERS = 2
ITEMS = LAYERS * B
FF = 512
FC = FF // P
EPS = 1e-5
SCALE = HD ** -0.5
MASKED = -1e30
HALF = H // 2
GROUPS = [(0, 0), (0, 1), (0, 2), (1, 0), (1, 1), (2, 0), (1, 2)]
NG = len(GROUPS)
SROWS = NG * HD
MROWS = SROWS + 3
VW = 32

ROWS = [("cond_1024", 4), ("L0_cond_bada", 6), ("L0_cond_g1", 1), ("L0_cond_be1", 1),
        ("L0_cond_g2", 1), ("L0_cond_be2", 1), ("L0_cond_b1", 4), ("L1_cond_w_norm1", 1),
        ("L1_cond_w_norm2", 1), ("L1_cond_t1_b1", 1), ("L1_cond_t2_b1", 1),
        ("L1_cond_t1_b2", 2), ("L1_cond_t2_b2", 2)]
NROWS = sum(n for _, n in ROWS)
COL = {name: sum(n for _, n in ROWS[:k]) for k, (name, _) in enumerate(ROWS)}


def score_units(i):
    units = []
    for qb in range(NT):
        keys = (qb + 1) * P if i < B else T
        n = 512 // keys
        units += [(qb, p, s, n, keys) for s in range(0, HALF, n) for p in range(2)]
    return units


def prob_units(i):
    if i < B:
        return [u for g in (0, 2) for u in
                [((g + k,), 0, p) for k in range(2) for p in range(2)] + [((g, g + 1), 1, p) for p in range(2)]]
    return [((g,), kb, p) for g in range(4) for kb in range(NT) for p in range(2)]


S_AT = [10, 22, 34, 46, 64, 80, 96, 112]
T_AT = [28, 40, 52, 64, 85, 101, 117, 133]
PRE_AT = [0, 4, 13, 25, 54, 67, 82, 98]
PV_LAG = 2


def items_plan():
    plan = {}

    def put(t, *steps):
        plan.setdefault(t, []).extend(steps)

    put(0, ("rows", 0))
    put(0, ("mods", 0))
    for i in range(ITEMS):
        a = PRE_AT[i]
        put(a, ("stats1", i))
        put(a + 1, ("turn1", i))
        put(a + 2, ("qk", i))
        if i >= B:
            put(a + 2, ("qk_rot", i))
        put(a + 3, ("v", i))
        put(S_AT[i] + len(score_units(i)) + 1, ("maxrows", i))
        c = T_AT[i] + len(prob_units(i)) + PV_LAG + (i < B)
        put(c, ("out_norm0", i))
        put(c + 1, ("out_norm1", i))
        put(c + 3, ("turn_out", i))
        put(c + 4, ("proj", i))
        put(c + 4, ("stats2", i))
        put(c + 6, ("turn2", i))
        if i < B:
            put(c + 8, ("hidden0", i))
            put(c + 8, ("hidden1", i))
        else:
            put(c + 7, ("gate0", i), ("up0", i))
            put(c + 8, ("gate1", i), ("up1", i))
        put(c + 10, ("down", i))
    put(3, ("gates0", 0))
    put(3, ("gates1", 0))
    put(8, ("times", 0))
    put(9, ("times2", 0))
    slots = max(plan) + 1
    return [plan.get(t, []) for t in range(slots)]


PLAN = items_plan()
SLOTS = len(PLAN)
S_UNITS = {S_AT[i] + n: (i, u) for i in range(ITEMS) for n, u in enumerate(score_units(i))}
T_UNITS = {T_AT[i] + n: (i, u) for i in range(ITEMS) for n, u in enumerate(prob_units(i))}
PV_AT = {}
for _i in range(ITEMS):
    for _n, (_gs, _kb, _p) in enumerate(prob_units(_i)):
        for _g in _gs:
            for _k in ((0, 1) if _i < B and _kb else (_kb,)):
                PV_AT[_i, _g, _k] = T_AT[_i] + _n + PV_LAG + (_g % 2 if _i < B else 0)
PV_SLOTS = {}
for _k, _t in sorted(PV_AT.items(), key=lambda kt: kt[0]):
    PV_SLOTS.setdefault(_t, []).append(_k)

BANK_STEPS = [(step, i) for steps in PLAN for step, i in steps if step not in ("stats1", "stats2")]
USE = {key: n for n, key in enumerate(BANK_STEPS)}


def s_number(i, n=0):
    return sum(len(score_units(j)) for j in range(i)) + n


def t_number(i, n=0):
    return sum(len(prob_units(j)) for j in range(i)) + n


def t_done(i, g, kb):
    return t_number(i) + max(n + 1 for n, u in enumerate(prob_units(i)) if g in u[0] and u[1] == kb)


def pv_number(i, g, kb):
    return (i * 4 + g) * NT + kb


def build(nc, a, out, consts):
    with ExitStack() as ctx:
        def sb(name, shape, dt=F32):
            return ctx.enter_context(nc.sbuf_tensor(name, shape, dt))

        def sem(name):
            return ctx.enter_context(nc.semaphore(name))

        banks = [ctx.enter_context(nc.psum_tensor(f"bank{k}", [P, 512], F32)) for k in range(8)]
        s_bank, t_bank, o_bank, m_bank = banks[0:2], banks[2:4], banks[4:6], banks[6:8]

        ident = sb("ident", [P, P])
        ident_bf = sb("ident_bf", [P, P], BF16)
        mask = sb("mask", [P, P])
        mask_bf = sb("mask_bf", [P, P], BF16)
        rope = sb("rope", [P, 2, T])
        rows = sb("rows", [NROWS, P])
        cols = sb("cols", [P, NROWS])
        w_qkv = sb("w_qkv", [P, 3, D])
        w_proj = sb("w_proj", [P, D])
        w_1 = sb("w_1", [P, FF])
        w_2 = sb("w_2", [P, FC, D])
        w_ada = sb("w_ada", [P, 6, D])
        w1_q, w1_k, w1_v, w1_o = (sb(f"w1_{n}", [P, D]) for n in "qkvo")
        w_gate = sb("w_gate", [P, FF])
        w_up = sb("w_up", [P, FF])
        w_down = sb("w_down", [P, FC, D])
        t_w1 = sb("t_w1", [P, 2, D])
        t_w2 = sb("t_w2", [P, 2, 2, D])
        bada_row = sb("bada_row", [P, 2, D])
        bproj_row = sb("bproj_row", [P, D])
        b2_row = sb("b2_row", [P, D])
        bv_row = sb("bv_row", [P, D])
        bo_row = sb("bo_row", [P, D])
        bqk_raw = sb("bqk_raw", [2, D])
        bqk_turned = sb("bqk_turned", [2, 2, D])
        bqk = sb("bqk", [P, 2, 2])
        w_qk = sb("w_qk", [P, LAYERS, 2, D])
        w_rot = sb("w_rot", [P, 2, D])
        silu = sb("silu", [P, 4, B])
        silu_wide = sb("silu_wide", [P, B, P])
        mod = sb("mod", [P, 4, B])
        gates = sb("gates", [P, 2, B, D])
        tsilu = sb("tsilu", [P, 5, 2, B])
        tmod = sb("tmod", [P, 2, 2, B])
        mul_c = sb("mul_c", [P, LAYERS, 2, B])
        add_c = sb("add_c", [P, LAYERS, 2, B])
        w_projg = sb("w_projg", [P, B, D])
        w_2g = sb("w_2g", [P, B, FC, D])
        add_attn = sb("add_attn", [P, B, D])
        add_mlp = sb("add_mlp", [P, B, D])
        xs = [sb(f"x{k}", [P, B * NT, D]) for k in range(2 * LAYERS + 1)]
        bn = sb("bn", [P, 2, NT, 6])
        mean_var = sb("mean_var", [P, 2, NT, 2])
        var_eps = sb("var_eps", [P, 2, 2, NT])
        rstd = sb("rstd", [P, 2, 2, NT])
        minus_half = sb("minus_half", [P, NT])
        square = sb("square", [P, NT])
        xn = [sb(f"xn{w}", [P, 2, NT, D]) for w in range(2)]
        x_bias = [sb(f"x_bias{w}", [P, 2, NT, D]) for w in range(2)]
        xmt = [sb(f"xmt{w}", [P, 2, T]) for w in range(2)]
        rot_a = sb("rot_a", [P, 2, T])
        rot_b = sb("rot_b", [P, 2, T])
        qk_full = sb("qk_full", [P, 2, T])
        rest = sb("rest", [P, 2, T])
        parts = sb("parts", [P, 2, 6, T], BF16)
        stacks = sb("stacks", [P, B, 2, HALF, T], BF16)
        v_sb = sb("v_sb", [P, B * NT, H, VW])
        row_max = sb("row_max", [P, 2, NT, 2, HALF])
        neg_max = sb("neg_max", [P, NT, 2, HALF])
        neg_rest = sb("neg_rest", [P, NT, 2, HALF])
        neg_parts = sb("neg_parts", [P, 2, NT, 2, 3, HALF], BF16)
        max_rows = sb("max_rows", [2 * 3 * HALF, 2, T], BF16)
        probs = sb("probs", [P, NT, H, T])
        o_t = sb("o_t", [P, 2, 4, T])
        denom = sb("denom", [P, NT, H])
        o_n = sb("o_n", [P, 2, NT, D])
        o_nt = sb("o_nt", [P, 2, T])
        gelu = sb("gelu", [P, 2, 2, T])
        hidden = sb("hidden", [P, 2, FC, T])
        scratch = nc.dram_tensor("stack_scratch", (2, 2, 2, SROWS * HALF, T), BF16, kind="Internal").ap()

        x_loaded = [sem(f"x_loaded{b}") for b in range(B)]
        consts_loaded = sem("consts_loaded")
        rows_loaded = sem("rows_loaded")
        w0_loaded = sem("w0_loaded")
        w0b_loaded = sem("w0b_loaded")
        w1_loaded = sem("w1_loaded")
        w1b_loaded = sem("w1b_loaded")
        casts_ready = sem("casts_ready")
        wqk0_ready = sem("wqk0_ready")
        wqk1_ready = sem("wqk1_ready")
        stacks_ones = sem("stacks_ones")
        v_ones = sem("v_ones")
        cols_ready = sem("cols_ready")
        neg_exp = sem("neg_exp")
        silu_ready = sem("silu_ready")
        norm0_ready = sem("norm0_ready")
        norm1_ready = sem("norm1_ready")
        wide_ready = sem("wide_ready")
        gates_ready = sem("gates_ready")
        gated_ready = sem("gated_ready")
        tz_ready = sem("tz_ready")
        texp_ready = sem("texp_ready")
        tsilu_ready = sem("tsilu_ready")
        vchain = sem("vchain")
        pchain = sem("pchain")
        stats_ready = [sem(f"stats_ready{w}") for w in range(2)]
        xn_ready = [sem(f"xn_ready{w}") for w in range(2)]
        x_bias_ready = [sem(f"x_bias_ready{w}") for w in range(2)]
        xmt_ready = [sem(f"xmt_ready{w}") for w in range(2)]
        bank_filled = sem("bank_filled")
        high_ready = sem("high_ready")
        rest_ready = sem("rest_ready")
        rot_ready = sem("rot_ready")
        parts_ready = sem("parts_ready")
        parts_stored = [sem(f"parts_stored{i}") for i in range(ITEMS)]
        stacks_loaded = [sem(f"stacks_loaded{i}") for i in range(ITEMS)]
        v_ready = sem("v_ready")
        s_filled = sem("s_filled")
        max_done = sem("max_done")
        negs_ready = sem("negs_ready")
        max_rows_ready = sem("max_rows_ready")
        max_rows_placed = [sem(f"max_rows_placed{i}") for i in range(ITEMS)]
        t_filled = sem("t_filled")
        exp_done = sem("exp_done")
        masked = sem("masked")
        pv_done = sem("pv_done")
        o_copied = sem("o_copied")
        on_ready = sem("on_ready")
        ont_ready = sem("ont_ready")
        mid_ready = sem("mid_ready")
        gelu_ready = sem("gelu_ready")
        hidden_ready = sem("hidden_ready")
        end_ready = sem("end_ready")
        out_stored = sem("out_stored")

        block = ctx.enter_context(nc.Block())

        def bank_of(step, i):
            return m_bank[USE[step, i] % 2]

        def filled(eng, step, i):
            eng.wait_ge(bank_filled, USE[step, i] + 1)

        def col(name, k=0):
            return cols[:, COL[name] + k:COL[name] + k + 1]

        @block.sync
        def _(sp):
            def load(dst, name_or_ap, signal):
                src = a[name_or_ap] if isinstance(name_or_ap, str) else name_or_ap
                sp.dma_start(dst, src).then_inc(signal, 16)

            def load_x(b):
                load(xs[0][:, b * NT:(b + 1) * NT, :], a["x"][b].rearrange("(j p) d -> p j d", p=P), x_loaded[b])

            load_x(0)
            for name, n in ROWS:
                src = a[name] if len(a[name].shape) == 2 else a[name].rearrange("(n d) -> n d", d=D)
                load(rows[COL[name]:COL[name] + n, :], src, rows_loaded)
            load(ident[:], consts["ident"], rows_loaded)
            load(w_qkv[:], a["L0_cond_Wqkv"].rearrange("p (k d) -> p k d", k=3), w0_loaded)
            load(w_ada[:], a["L0_cond_Wada"].rearrange("p (k d) -> p k d", k=6), w0_loaded)
            load(mask[:], consts["mask"], consts_loaded)
            load_x(1)
            load(bada_row[:, 0, :], a["L0_cond_bada"][2 * D:3 * D].partition_broadcast(P), w0b_loaded)
            load(bada_row[:, 1, :], a["L0_cond_bada"][5 * D:6 * D].partition_broadcast(P), w0b_loaded)
            load(bproj_row[:], a["L0_cond_bproj"].partition_broadcast(P), w0b_loaded)
            load(b2_row[:], a["L0_cond_b2"].partition_broadcast(P), w0b_loaded)
            load(w_proj[:], "L0_cond_Wproj", w0b_loaded)
            load(w_1[:], "L0_cond_W1", w0b_loaded)
            load(w_2[:], a["L0_cond_W2"].rearrange("(c p) d -> p c d", p=P), w0b_loaded)
            load_x(2)
            load_x(3)

            def load_layer1():
                load(rope[:], consts["rope"], w1_loaded)
                load(w1_q[:], "L1_cond_wq", w1_loaded)
                load(w1_k[:], "L1_cond_wk", w1_loaded)
                load(t_w1[:, 0, :], "L1_cond_t1_w1", w1_loaded)
                load(t_w1[:, 1, :], "L1_cond_t2_w1", w1_loaded)
                load(t_w2[:, 0, :, :], a["L1_cond_t1_w2"].rearrange("p (k d) -> p k d", k=2), w1_loaded)
                load(t_w2[:, 1, :, :], a["L1_cond_t2_w2"].rearrange("p (k d) -> p k d", k=2), w1_loaded)
                load(bqk_raw[0:1, :], a["L1_cond_bq"].rearrange("(n d) -> n d", d=D), w1_loaded)
                load(bqk_raw[1:2, :], a["L1_cond_bk"].rearrange("(n d) -> n d", d=D), w1_loaded)
                load(w1_v[:], "L1_cond_wv", w1b_loaded)
                load(w1_o[:], "L1_cond_wo", w1b_loaded)
                load(w_gate[:], "L1_cond_w_gate", w1b_loaded)
                load(w_up[:], "L1_cond_w_up", w1b_loaded)
                load(w_down[:], a["L1_cond_w_down"].rearrange("(c p) d -> p c d", p=P), w1b_loaded)
                load(bv_row[:], a["L1_cond_bv"].partition_broadcast(P), w1b_loaded)
                load(bo_row[:], a["L1_cond_bo"].partition_broadcast(P), w1b_loaded)

            def make_stacks(i):
                b, buf = i % B, i % 2
                sp.wait_ge(parts_ready, i + 1)
                if i >= 2:
                    sp.wait_ge(stacks_loaded[i - 2], 32)
                for g, (pq, pk) in enumerate(GROUPS):
                    for p in range(2):
                        sp.dma_start(
                            scratch[buf, :, p, g * 64:(g + 1) * 64, :].rearrange("k r t -> r k t"),
                            parts[64 * p:64 * p + 64, buf, pq:4 + pk:3 + pk - pq, :],
                        ).then_inc(parts_stored[i], 16)
                sp.wait_ge(parts_stored[i], 16 * 2 * NG)
                if i == 0:
                    sp.wait_ge(stacks_ones, 1)
                if i >= B:
                    sp.wait_ge(s_filled, s_number(i - B + 1))
                    sp.wait_ge(t_filled, t_number(i - B + 1))
                for p in range(2):
                    sp.dma_start(
                        stacks[64 * p:64 * p + SROWS, b, :, :, :].rearrange("r k s t -> r k (s t)"),
                        scratch[buf, :, p].rearrange("k (r s) t -> r k (s t)", s=HALF),
                    ).then_inc(stacks_loaded[i], 16)

            for steps in PLAN:
                for step, i in steps:
                    if step == "v":
                        make_stacks(i)
                        if i == 0:
                            load_layer1()
                    if step == "down" and i >= B:
                        b = i % B
                        sp.wait_ge(end_ready, i + 1)
                        sp.dma_start(out[b].rearrange("(j p) d -> p j d", p=P),
                                     xs[4][:, b * NT:(b + 1) * NT, :]).then_inc(out_stored, 16)
            sp.wait_ge(out_stored, 16 * B)

        @block.tensor
        def _(pe):
            def reader_of(step, i):
                k = int(step[-1]) if step[-1].isdigit() else 0
                if step in ("turn1", "turn2"):
                    return xmt_ready[k - 1], i + 1
                return {
                    "rows": (cols_ready, 1), "mods": (norm0_ready, 1), "gates": (gates_ready, k + 1),
                    "times": (norm1_ready if k else tz_ready, 1),
                    "qk": (rot_ready, 2 * (i - B) + 1) if i >= B else (rest_ready, i + 1),
                    "qk_rot": (rot_ready, 2 * (i - B) + 2), "v": (v_ready, i + 1),
                    "maxrows": (max_rows_ready, i + 1), "out_norm": (on_ready, NT * i + k + 1),
                    "turn_out": (ont_ready, i + 1), "proj": (mid_ready, i + 1),
                    "hidden": (hidden_ready, 2 * i + k + 1), "gate": (gelu_ready, 2 * (i - B) + k + 1),
                    "up": (hidden_ready, 2 * i + k + 1), "down": (end_ready, i + 1),
                }[step.rstrip("012")]

            def take_bank(step, i):
                n = USE[step, i]
                if n >= 2:
                    pe.wait_ge(*reader_of(*BANK_STEPS[n - 2]))
                return m_bank[n % 2]

            def mm(o, lhs, rhs, start=True, stop=True):
                return pe.matmul(o, lhs, rhs, start=start, stop=stop)

            def rows_to_cols():
                bank = take_bank("rows", 0)
                pe.wait_ge(rows_loaded, 16 * (len(ROWS) + 1))
                pe.transpose(bank[:, 0:NROWS], rows[:], ident[0:NROWS, 0:NROWS]).then_inc(bank_filled, 1)

            def mods():
                bank = take_bank("mods", 0)
                pe.wait_ge(silu_ready, 1)
                pe.wait_ge(w0_loaded, 32)
                for n, chunk in enumerate((0, 1, 3, 4)):
                    last = mm(bank[:, n * B:(n + 1) * B], w_ada[:, chunk, :], silu[:, 3, :])
                last.then_inc(bank_filled, 1)

            def gate_rows(k):
                bank = take_bank(f"gates{k}", 0)
                pe.wait_ge(wide_ready, 1)
                for b in range(B):
                    last = mm(bank[:, b * D:(b + 1) * D], silu_wide[:, b, :], w_ada[:, 2 + 3 * k, :])
                last.then_inc(bank_filled, 1)

            def times():
                bank = take_bank("times", 0)
                pe.wait_ge(w1_loaded, 16 * 9)
                pe.wait_ge(wqk1_ready, 1)
                for k in range(2):
                    mm(bank[:, k * B:(k + 1) * B], t_w1[:, k, :], cols[:, 0:B])
                for k in range(2):
                    last = pe.transpose(bank[:, 16 + 2 * k:18 + 2 * k], bqk_turned[:, k, :], ident[0:2, 0:2])
                last.then_inc(bank_filled, 1)

            def times2():
                bank = take_bank("times2", 0)
                pe.wait_ge(tsilu_ready, 1)
                for k in range(2):
                    for n in range(2):
                        last = mm(bank[:, (2 * k + n) * B:(2 * k + n + 1) * B], t_w2[:, k, n, :], tsilu[:, 4, k, :])
                last.then_inc(bank_filled, 1)

            def turn(w, i):
                bank = take_bank(f"turn{w + 1}", i)
                for j in range(NT):
                    pe.wait_ge(xn_ready[w], NT * i + j + 1)
                    last = pe.transpose(bank[:, j * P:(j + 1) * P], xn[w][:, i % 2, j, :], ident[:])
                last.then_inc(bank_filled, 1)

            def project_qk(i, rotated=False):
                layer = i // B
                bank = take_bank("qk_rot" if rotated else "qk", i)
                pe.wait_ge(xmt_ready[0], i + 1)
                pe.wait_ge(wqk1_ready if layer else wqk0_ready, 1)
                for k in range(2):
                    w = w_rot[:, k, :] if rotated else w_qk[:, layer, k, :]
                    last = mm(bank[:, k * T:(k + 1) * T], w, xmt[0][:, i % 2, :])
                last.then_inc(bank_filled, 1)

            def project_v(i):
                bank = take_bank("v", i)
                if i == B:
                    pe.wait_ge(w1b_loaded, 16 * 7)
                w = w1_v[:] if i >= B else w_qkv[:, 2, :]
                for j in range(NT):
                    last = mm(bank[:, j * D:(j + 1) * D], xmt[0][:, i % 2, j * P:(j + 1) * P], w)
                last.then_inc(bank_filled, 1)

            def scores(i, n, unit):
                qb, p, s0, heads, keys = unit
                b, number = i % B, s_number(i, n)
                bank = s_bank[number % 2]
                if n == 0:
                    pe.wait_ge(stacks_loaded[i], 32)
                if number == 0:
                    pe.wait_ge(casts_ready, 2)
                if number >= 2:
                    pe.wait_ge(max_done, number - 1)
                r = slice(64 * p, 64 * p + SROWS)
                for k in range(heads):
                    o = bank[:, k * keys:(k + 1) * keys]
                    last = mm(o, stacks[r, b, 0, s0 + k, qb * P:(qb + 1) * P], stacks[r, b, 1, s0 + k, 0:keys],
                              stop=i >= B)
                    if i < B:
                        last = mm(o[:, keys - P:keys], ident_bf[:], mask_bf[:], start=False)
                last.then_inc(s_filled, 1)

            def place_max(i):
                bank = take_bank("maxrows", i)[:].bitcast(BF16)
                pe.wait_ge(negs_ready, i + 1)
                for qb in range(NT):
                    last = pe.transpose(bank[0:48, qb * P:(qb + 1) * P],
                                        neg_parts[:, i % 2, qb].rearrange("q p n s -> q (p n s)"), ident_bf[:])
                last.then_inc(bank_filled, 1)

            def scores_t(i, n, unit):
                gs, kb, parity = unit
                b, number = i % B, t_number(i, n)
                bank = t_bank[number % 2]
                if n == 0:
                    pe.wait_ge(max_rows_placed[i], 16 * 6)
                if number >= 2:
                    pe.wait_ge(exp_done, number - 1)
                q0 = (len(gs) - 1) * P
                for k, (g, j) in enumerate((g, j) for g in gs for j in (parity, parity + 2)):
                    p, s = j % 2, 2 * g + j // 2
                    r = slice(64 * p, 64 * p + MROWS)
                    last = mm(bank[:, k * (T - q0):(k + 1) * (T - q0)],
                              stacks[r, b, 1, s, kb * P:(kb + 1) * P], stacks[r, b, 0, s, q0:T])
                last.then_inc(t_filled, 1)

            def pv(i, g, kb):
                b = i % B
                if g == 0 and kb == 0:
                    pe.wait_ge(v_ready, i + 1)
                if g % 2 == 0 and kb == 0 and 2 * i + g // 2 >= 2:
                    pe.wait_ge(o_copied, 2 * i + g // 2 - 1)
                if i < B:
                    pe.wait_ge(masked, t_done(i, g, kb))
                else:
                    pe.wait_ge(exp_done, t_done(i, g, kb))
                q0 = P if i < B and kb == 1 else 0
                bank = o_bank[g // 2]
                for j in range(4):
                    last = pe.matmul(bank[32 * j:32 * j + VW, (g % 2) * T + q0:(g % 2 + 1) * T],
                                     v_sb[:, b * NT + kb, 4 * g + j, :], probs[:, kb, 4 * g + j, q0:T],
                                     start=(kb == 0), stop=(kb == NT - 1), tile_position=(0, 32 * j))
                last.then_inc(pv_done, 1)

            def out_turn(i, qb):
                bank = take_bank(f"out_norm{qb}", i)
                pe.wait_ge(o_copied, 2 * (i + 1))
                for g in range(4):
                    last = pe.transpose(bank[:, g * P:(g + 1) * P], o_t[:, i % 2, g, qb * P:(qb + 1) * P], ident[:])
                last.then_inc(bank_filled, 1)

            def turn_out(i):
                bank = take_bank("turn_out", i)
                for j in range(NT):
                    pe.wait_ge(on_ready, NT * i + j + 1)
                    last = pe.transpose(bank[:, j * P:(j + 1) * P], o_n[:, i % 2, j, :], ident[:])
                last.then_inc(bank_filled, 1)

            def project_out(i):
                bank = take_bank("proj", i)
                if i == 0:
                    pe.wait_ge(gated_ready, 1)
                pe.wait_ge(ont_ready, i + 1)
                w = w1_o[:] if i >= B else w_projg[:, i % B, :]
                for j in range(NT):
                    last = mm(bank[:, j * D:(j + 1) * D], o_nt[:, i % 2, j * P:(j + 1) * P], w)
                last.then_inc(bank_filled, 1)

            def mlp_in(step, i, w):
                half = int(step[-1])
                bank = take_bank(step, i)
                pe.wait_ge(xmt_ready[1], i + 1)
                for k in range(2):
                    c = 2 * half + k
                    last = mm(bank[:, k * T:(k + 1) * T], w[:, c * P:(c + 1) * P], xmt[1][:, i % 2, :])
                last.then_inc(bank_filled, 1)

            def mlp_out(i):
                bank = take_bank("down", i)
                if i == 0:
                    pe.wait_ge(gated_ready, 2)
                pe.wait_ge(hidden_ready, 2 * (i + 1))
                for j in range(NT):
                    for c in range(FC):
                        w = w_down[:, c, :] if i >= B else w_2g[:, i % B, c, :]
                        last = mm(bank[:, j * D:(j + 1) * D], hidden[:, i % 2, c, j * P:(j + 1) * P], w,
                                  start=(c == 0), stop=(c == FC - 1))
                last.then_inc(bank_filled, 1)

            for t in range(SLOTS):
                if t in T_UNITS:
                    i, unit = T_UNITS[t]
                    scores_t(i, t - T_AT[i], unit)
                for i, g, kb in PV_SLOTS.get(t, ()):
                    pv(i, g, kb)
                for step, i in PLAN[t]:
                    if step == "rows":
                        rows_to_cols()
                    elif step == "mods":
                        mods()
                    elif step.startswith("gates"):
                        gate_rows(int(step[-1]))
                    elif step == "times":
                        times()
                    elif step == "times2":
                        times2()
                    elif step in ("turn1", "turn2"):
                        turn(int(step[-1]) - 1, i)
                    elif step == "qk":
                        project_qk(i)
                    elif step == "qk_rot":
                        project_qk(i, rotated=True)
                    elif step == "v":
                        project_v(i)
                    elif step == "maxrows":
                        place_max(i)
                    elif step.startswith("out_norm"):
                        out_turn(i, int(step[-1]))
                    elif step == "turn_out":
                        turn_out(i)
                    elif step == "proj":
                        project_out(i)
                    elif step.startswith("hidden"):
                        mlp_in(step, i, w_1)
                    elif step.startswith("gate"):
                        mlp_in(step, i, w_gate)
                    elif step.startswith("up"):
                        mlp_in(step, i, w_up)
                    elif step == "down":
                        mlp_out(i)
                if t in S_UNITS:
                    i, unit = S_UNITS[t]
                    scores(i, t - S_AT[i], unit)

        @block.scalar
        def _(act):
            def affine(w, i):
                layer, b = divmod(i, B)
                step = f"turn{w + 1}"
                if i == 0 and w == 0:
                    act.wait_ge(norm0_ready, 1)
                if i == B and w == 0:
                    act.wait_ge(norm1_ready, 1)
                if i >= 2:
                    filled(act, ("v" if w == 0 else "hidden1" if i - 2 < B else "up1"), i - 2)
                filled(act, step, i)
                ins = act.activation(xmt[w][:, i % 2, :], bank_of(step, i)[:, 0:T], ACT.Identity,
                                     bias=add_c[:, layer, w, b:b + 1], scale=mul_c[:, layer, w, b:b + 1])
                ins.then_inc(xmt_ready[w], 1)

            def high_part(i):
                if i >= 2:
                    act.wait_ge(parts_stored[i - 2], 16 * 2 * NG)
                filled(act, "qk", i)
                act.activation(parts[:, i % 2, 0:4:3, :], bank_of("qk", i)[:].rearrange("c (k t) -> c k t", k=2),
                               ACT.Copy).then_inc(high_ready, 1)

            def copy_v(i):
                b = i % B
                if i == 0:
                    act.wait_ge(v_ones, 1)
                filled(act, "v", i)
                ins = act.activation(v_sb[:, b * NT:(b + 1) * NT, :, 0:HD],
                                     bank_of("v", i)[:, 0:T].rearrange("k (j h d) -> k j h d", j=NT, h=H), ACT.Copy)
                ins.then_inc(v_ready, 1)

            def move_max(i):
                b = i % B
                if i >= 2:
                    act.wait_ge(max_rows_placed[i - 2], 16 * 6)
                filled(act, "maxrows", i)
                ins = act.activation(max_rows[:, i % 2, :], bank_of("maxrows", i)[:].bitcast(BF16)[0:48, 0:T], ACT.Copy)
                ins.then_inc(max_rows_ready, 1)
                act.wait_ge(max_rows_ready, i + 1)
                for p in range(2):
                    for n in range(3):
                        r = (p * 3 + n) * HALF
                        row = 64 * p + SROWS + n
                        act.dma_start(stacks[row:row + 1, b, 0, :, :],
                                      max_rows[r:r + HALF, i % 2, :]).then_inc(max_rows_placed[i], 16)

            def exponentials(i, n, unit):
                gs, kb, parity = unit
                if i >= 1:
                    act.wait_ge(pv_done, pv_number(i, gs[-1], kb) - 4 * NT + 1)
                number = t_number(i, n)
                act.wait_ge(t_filled, number + 1)
                q0 = (len(gs) - 1) * P
                dst = probs[:, kb, 4 * gs[0] + parity:4 * gs[-1] + 4:2, q0:T]
                src = t_bank[number % 2][:].rearrange("k (h q) -> k h q", h=2 * len(gs))
                act.activation(dst, src, ACT.Exp, scale=SCALE).then_inc(exp_done, 1)

            def copy_o(i, pair):
                if i >= 2:
                    filled(act, "out_norm1", i - 2)
                act.wait_ge(pv_done, pv_number(i, 2 * pair + 1, 1) + 1)
                act.activation(o_t[:, i % 2, 2 * pair:2 * pair + 2, :],
                               o_bank[pair][:].rearrange("r (g q) -> r g q", g=2), ACT.Copy).then_inc(o_copied, 1)

            def copy_ont(i):
                if i >= 2:
                    filled(act, "proj", i - 2)
                filled(act, "turn_out", i)
                ins = act.activation(o_nt[:, i % 2, :], bank_of("turn_out", i)[:, 0:T], ACT.Copy)
                ins.then_inc(ont_ready, 1)

            def hidden_gelu(step, i):
                half = int(step[-1])
                if i >= 2 and half == 0:
                    filled(act, "down", i - 2)
                filled(act, step, i)
                for k in range(2):
                    c = 2 * half + k
                    ins = act.activation(hidden[:, i % 2, c, :], bank_of(step, i)[:, k * T:(k + 1) * T],
                                         ACT.Gelu, bias=col("L0_cond_b1", c))
                ins.then_inc(hidden_ready, 1)

            def gate_gelu(step, i):
                half = int(step[-1])
                if 2 * (i - B) + half >= 2:
                    act.wait_ge(hidden_ready, 2 * i + half - 1)
                filled(act, step, i)
                act.activation(gelu[:, half, :, :], bank_of(step, i)[:].rearrange("f (k t) -> f k t", k=2),
                               ACT.Gelu).then_inc(gelu_ready, 1)

            act.wait_ge(cols_ready, 1)
            act.activation(silu[:, 0, :], cols[:, 0:B], ACT.Exp, scale=-1.0).then_inc(neg_exp, 1)
            for t in range(SLOTS):
                if t in T_UNITS:
                    i, unit = T_UNITS[t]
                    exponentials(i, t - T_AT[i], unit)
                for i, g, kb in PV_SLOTS.get(t, ()):
                    if g % 2 == 1 and kb == 1:
                        copy_o(i, g // 2)
                for step, i in PLAN[t]:
                    if step in ("turn1", "turn2"):
                        affine(int(step[-1]) - 1, i)
                    elif step == "qk" and i < B:
                        high_part(i)
                    elif step == "v" and i < B:
                        copy_v(i)
                    elif step == "maxrows":
                        move_max(i)
                    elif step == "turn_out":
                        copy_ont(i)
                    elif step.startswith("hidden"):
                        hidden_gelu(step, i)
                    elif step in ("gate0", "gate1"):
                        gate_gelu(step, i)
                    elif step == "times":
                        act.wait_ge(tz_ready, 1)
                        act.activation(tsilu[:, 1, :, :], tsilu[:, 0, :, :], ACT.Exp, scale=-1.0).then_inc(texp_ready, 1)

        @block.vector
        def _(dve):
            links = [0]

            def link(ins):
                links[0] += 1
                ins.then_inc(vchain, 1)
                dve.wait_ge(vchain, links[0])

            def cond_silu():
                filled(dve, "rows", 0)
                dve.tensor_copy(cols[:], bank_of("rows", 0)[:, 0:NROWS]).then_inc(cols_ready, 1)
                dve.wait_ge(neg_exp, 1)
                link(dve.tensor_scalar_add(silu[:, 1, :], silu[:, 0, :], 1.0))
                link(dve.reciprocal(silu[:, 2, :], silu[:, 1, :]))
                dve.tensor_tensor(silu[:, 3, :], silu[:, 2, :], cols[:, 0:B], ALU.mult).then_inc(silu_ready, 1)
                dve.wait_ge(silu_ready, 1)
                dve.tensor_copy(silu_wide[:], silu[:, 3, :].unsqueeze(2).to_broadcast([P, B, P])).then_inc(wide_ready, 1)

            def norm_mods():
                filled(dve, "mods", 0)
                for n, chunk in enumerate((0, 1, 3, 4)):
                    ins = dve.tensor_scalar(mod[:, n, :], bank_of("mods", 0)[:, n * B:(n + 1) * B],
                                            col("L0_cond_bada", chunk), float(n % 2), ALU.add, ALU.add)
                link(ins)
                for w in range(2):
                    dve.tensor_scalar(mul_c[:, 0, w, :], mod[:, 2 * w + 1, :], col(f"L0_cond_g{w + 1}"), None, ALU.mult)
                    ins = dve.scalar_tensor_tensor(add_c[:, 0, w, :], mod[:, 2 * w + 1, :], col(f"L0_cond_be{w + 1}"),
                                                   mod[:, 2 * w, :], ALU.mult, ALU.add)
                ins.then_inc(norm0_ready, 1)

            def gate_rows(k):
                step = f"gates{k}"
                if k == 0:
                    dve.wait_ge(w0b_loaded, 16 * 7)
                filled(dve, step, 0)
                dve.tensor_tensor(gates[:, k, :, :], bank_of(step, 0)[:].rearrange("p (b d) -> p b d", b=B),
                                  bada_row[:, k, :].unsqueeze(1).to_broadcast([P, B, D]), ALU.add).then_inc(gates_ready, 1)

            def times():
                filled(dve, "times", 0)
                bank = bank_of("times", 0)
                dve.tensor_copy(bqk[:], bank[:, 16:20].rearrange("p (n k) -> p n k", n=2))
                for k in range(2):
                    ins = dve.tensor_scalar(tsilu[:, 0, k, :], bank[:, k * B:(k + 1) * B], col(f"L1_cond_t{k + 1}_b1"),
                                            None, ALU.add)
                ins.then_inc(tz_ready, 1)
                dve.wait_ge(texp_ready, 1)
                link(dve.tensor_scalar_add(tsilu[:, 2, :, :], tsilu[:, 1, :, :], 1.0))
                link(dve.reciprocal(tsilu[:, 3, :, :], tsilu[:, 2, :, :]))
                dve.tensor_tensor(tsilu[:, 4, :, :], tsilu[:, 3, :, :], tsilu[:, 0, :, :], ALU.mult).then_inc(tsilu_ready, 1)

            def times2():
                filled(dve, "times2", 0)
                bank = bank_of("times2", 0)
                for k in range(2):
                    ins = dve.tensor_scalar(tmod[:, k, 0, :], bank[:, 2 * k * B:(2 * k + 1) * B],
                                            col(f"L1_cond_t{k + 1}_b2", 0), 1.0, ALU.add, ALU.add)
                    dve.tensor_scalar(add_c[:, 1, k, :], bank[:, (2 * k + 1) * B:(2 * k + 2) * B],
                                      col(f"L1_cond_t{k + 1}_b2", 1), None, ALU.add)
                link(ins)
                for k in range(2):
                    ins = dve.tensor_scalar(mul_c[:, 1, k, :], tmod[:, k, 0, :], col(f"L1_cond_w_norm{k + 1}"),
                                            None, ALU.mult)
                ins.then_inc(norm1_ready, 1)

            def stats(w, i):
                layer, b = divmod(i, B)
                if w == 0:
                    if layer == 0:
                        dve.wait_ge(x_loaded[b], 16)
                    else:
                        dve.wait_ge(end_ready, i - B + 1)
                else:
                    dve.wait_ge(mid_ready, i + 1)
                if i >= 2:
                    dve.wait_ge(xn_ready[w], NT * (i - 1))
                x = xs[2 * layer + w]
                for j in range(NT):
                    ins = dve.bn_stats(bn[:, w, j, :], x[:, b * NT + j, :])
                link(ins)
                mv = mean_var[:, w]
                if i >= 1:
                    dve.wait_ge(xn_ready[w], NT * i)
                for j in range(NT):
                    ins = dve.bn_aggr(mv[:, j, :], bn[:, w, j, :])
                link(ins)
                if layer:
                    link(dve.tensor_tensor(square[:], mv[:, :, 0], mv[:, :, 0], ALU.mult))
                    ins = dve.scalar_tensor_tensor(var_eps[:, w, i % 2, :], square[:], EPS, mv[:, :, 1], ALU.add, ALU.add)
                else:
                    ins = dve.tensor_scalar_add(var_eps[:, w, i % 2, :], mv[:, :, 1], EPS)
                ins.then_inc(stats_ready[w], 1)

            def rest_of_qk(i):
                if i >= 1:
                    dve.wait_ge(parts_ready, i)
                dve.wait_ge(high_ready, i + 1)
                ins = dve.tensor_tensor(rest[:], bank_of("qk", i)[:].rearrange("c (k t) -> c k t", k=2),
                                        parts[:, i % 2, 0:4:3, :], ALU.subtract)
                ins.then_inc(rest_ready, 1)

            def rotate(i, sines):
                step = "qk_rot" if sines else "qk"
                if i > B and not sines:
                    dve.wait_ge(parts_ready, i)
                filled(dve, step, i)
                dst = rot_b if sines else rot_a
                for k in range(2):
                    ins = dve.scalar_tensor_tensor(dst[:, k, :], bank_of(step, i)[:, k * T:(k + 1) * T],
                                                   bqk[:, int(sines), k:k + 1], rope[:, int(sines), :], ALU.add, ALU.mult)
                ins.then_inc(rot_ready, 1)

            def add_bv(i):
                b = i % B
                dve.wait_ge(pv_done, pv_number(i - B, 3, 1) + 1)
                if i == B:
                    dve.wait_ge(w1b_loaded, 16 * 7)
                filled(dve, "v", i)
                ins = dve.tensor_tensor(v_sb[:, b * NT:(b + 1) * NT, :, 0:HD],
                                        bank_of("v", i)[:, 0:T].rearrange("k (j h d) -> k j h d", j=NT, h=H),
                                        bv_row[:].rearrange("k (h d) -> k h d", h=H).unsqueeze(1)
                                        .to_broadcast([P, NT, H, HD]), ALU.add)
                ins.then_inc(v_ready, 1)

            def maxima(i, n, unit):
                qb, p, s0, heads, keys = unit
                number = s_number(i, n)
                if n == 0 and i >= 2:
                    dve.wait_ge(negs_ready, i - 1)
                dve.wait_ge(s_filled, number + 1)
                dve.tensor_reduce(row_max[:, i % 2, qb, p, s0:s0 + heads],
                                  s_bank[number % 2][:].rearrange("q (s k) -> q s k", s=heads), AX_X, ALU.max)\
                   .then_inc(max_done, 1)

            def normalise(i, qb):
                step = f"out_norm{qb}"
                filled(dve, step, i)
                if i >= 2 and qb == 0:
                    filled(dve, "turn_out", i - 2)
                o = bank_of(step, i)[:].rearrange("q (h w) -> q h w", h=H)
                link(dve.reciprocal(denom[:, qb, :], o[:, :, HD]))
                ins = dve.tensor_tensor(o_n[:, i % 2, qb, :].rearrange("q (h d) -> q h d", h=H), o[:, :, 0:HD],
                                        denom[:, qb, :].unsqueeze(2).to_broadcast([P, H, HD]), ALU.mult)
                ins.then_inc(on_ready, 1)

            def add_attention(i):
                layer, b = divmod(i, B)
                filled(dve, "proj", i)
                dve.wait_ge(x_bias_ready[0], i + 1)
                dve.tensor_tensor(xs[2 * layer + 1][:, b * NT:(b + 1) * NT, :],
                                  bank_of("proj", i)[:, 0:T].rearrange("t (j d) -> t j d", j=NT),
                                  x_bias[0][:, i % 2, :, :], ALU.add).then_inc(mid_ready, 1)

            def times_up(step, i):
                half = int(step[-1])
                if half == 0:
                    filled(dve, "down", i - 2)
                filled(dve, step, i)
                dve.wait_ge(gelu_ready, 2 * (i - B) + half + 1)
                dve.tensor_tensor(hidden[:, i % 2, 2 * half:2 * half + 2, :],
                                  bank_of(step, i)[:].rearrange("f (k t) -> f k t", k=2), gelu[:, half, :, :],
                                  ALU.mult).then_inc(hidden_ready, 1)

            def add_mlp_out(i):
                layer, b = divmod(i, B)
                filled(dve, "down", i)
                if layer == 0:
                    dve.wait_ge(x_bias_ready[1], i + 1)
                old = xs[3][:, b * NT:(b + 1) * NT, :] if layer else x_bias[1][:, i % 2, :, :]
                dve.tensor_tensor(xs[2 * layer + 2][:, b * NT:(b + 1) * NT, :],
                                  bank_of("down", i)[:, 0:T].rearrange("t (j d) -> t j d", j=NT),
                                  old, ALU.add).then_inc(end_ready, 1)

            for t in range(SLOTS):
                for step, i in PLAN[t]:
                    if step == "rows":
                        cond_silu()
                    elif step == "mods":
                        norm_mods()
                    elif step.startswith("gates"):
                        gate_rows(int(step[-1]))
                    elif step == "times":
                        times()
                    elif step == "times2":
                        times2()
                    elif step in ("stats1", "stats2"):
                        stats(int(step[-1]) - 1, i)
                    elif step == "qk":
                        rotate(i, False) if i >= B else rest_of_qk(i)
                    elif step == "qk_rot":
                        rotate(i, True)
                    elif step == "v" and i >= B:
                        add_bv(i)
                    elif step.startswith("out_norm"):
                        normalise(i, int(step[-1]))
                    elif step == "proj":
                        add_attention(i)
                    elif step.startswith("up"):
                        times_up(step, i)
                    elif step == "down":
                        add_mlp_out(i)
                if t in S_UNITS:
                    i, unit = S_UNITS[t]
                    maxima(i, t - S_AT[i], unit)

        @block.gpsimd
        def _(pool):
            links = [0]

            def link(ins):
                links[0] += 1
                ins.then_inc(pchain, 1)
                pool.wait_ge(pchain, links[0])

            def by_parity(w):
                return w.rearrange("i (s p d) -> i p d s", p=2, d=HD)

            def in_order(w):
                return w.rearrange("i (p d s) -> i p d s", p=2, d=HD)

            def setup0():
                pool.memset(stacks[:, :, 1, :, :], 1.0).then_inc(stacks_ones, 1)
                pool.wait_ge(w0_loaded, 32)
                for k in range(2):
                    ins = [pool.tensor_copy(in_order(w_qk[:, 0, k, :])[:, p], by_parity(w_qkv[:, k, :])[:, p])
                           for p in range(2)][-1]
                ins.then_inc(wqk0_ready, 1)
                pool.memset(minus_half[:], -0.5)
                link(pool.memset(v_sb[:], 0.0))
                pool.memset(v_sb[:, :, :, HD:HD + 1], 1.0).then_inc(v_ones, 1)
                pool.wait_ge(rows_loaded, 16 * (len(ROWS) + 1))
                pool.tensor_copy(ident_bf[:], ident[:]).then_inc(casts_ready, 1)
                pool.wait_ge(consts_loaded, 16)
                pool.tensor_copy(mask_bf[:], mask[:]).then_inc(casts_ready, 1)

            def setup_gated():
                pool.wait_ge(gates_ready, 2)
                pool.tensor_tensor(w_projg[:], gates[:, 0, :, :], w_proj[:].unsqueeze(1).to_broadcast([P, B, D]), ALU.mult)
                link(pool.tensor_tensor(add_attn[:], gates[:, 0, :, :], bproj_row[:].unsqueeze(1).to_broadcast([P, B, D]),
                                        ALU.mult))
                ins = pool.tensor_tensor(add_mlp[:], gates[:, 1, :, :], b2_row[:].unsqueeze(1).to_broadcast([P, B, D]),
                                         ALU.mult)
                ins.then_inc(gated_ready, 1)
                for b in range(B):
                    ins = pool.tensor_tensor(w_2g[:, b, :, :], w_2[:], gates[:, 1, b, :].unsqueeze(1)
                                             .to_broadcast([P, FC, D]), ALU.mult)
                ins.then_inc(gated_ready, 1)

            def setup1():
                pool.wait_ge(w1_loaded, 16 * 9)
                lo, hi = slice(0, HD // 2), slice(HD // 2, HD)
                for k, w in enumerate((w1_q, w1_k)):
                    for p in range(2):
                        src = by_parity(w[:])[:, p]
                        dst, rot = in_order(w_qk[:, 1, k, :])[:, p], in_order(w_rot[:, k, :])[:, p]
                        pool.tensor_copy(dst, src)
                        pool.tensor_copy(rot[:, hi], src[:, lo])
                        pool.tensor_scalar(rot[:, lo], src[:, hi], -1.0, None, ALU.mult)
                for p in range(2):
                    src = by_parity(bqk_raw[:])[:, p]
                    dst, rot = in_order(bqk_turned[:, 0, :])[:, p], in_order(bqk_turned[:, 1, :])[:, p]
                    pool.tensor_copy(dst, src)
                    pool.tensor_copy(rot[:, hi], src[:, lo])
                    ins = pool.tensor_scalar(rot[:, lo], src[:, hi], -1.0, None, ALU.mult)
                ins.then_inc(wqk1_ready, 1)

            def centre(w, i):
                layer, b = divmod(i, B)
                x = xs[2 * layer + w]
                if i >= 2:
                    filled(pool, f"turn{w + 1}", i - 2)
                pool.wait_ge(stats_ready[w], i + 1)
                link(pool.tensor_tensor(rstd[:, w, i % 2, :], var_eps[:, w, i % 2, :], minus_half[:], ALU.pow))
                for j in range(NT):
                    scale = rstd[:, w, i % 2, j:j + 1]
                    if layer == 0:
                        ins = pool.tensor_scalar(xn[w][:, i % 2, j, :], x[:, b * NT + j, :], mean_var[:, w, j, 0:1], scale,
                                                 ALU.subtract, ALU.mult)
                    else:
                        ins = pool.tensor_scalar(xn[w][:, i % 2, j, :], x[:, b * NT + j, :], scale, None, ALU.mult)
                    ins.then_inc(xn_ready[w], 1)

            def add_bias(w, i):
                layer, b = divmod(i, B)
                if layer and w:
                    return
                if i >= 2:
                    pool.wait_ge(end_ready if w else mid_ready, i - 1)
                if i == 0 and w == 0:
                    pool.wait_ge(gated_ready, 1)
                if i == B:
                    pool.wait_ge(w1b_loaded, 16 * 7)
                bias = bo_row[:] if layer else (add_mlp if w else add_attn)[:, b, :]
                pool.tensor_tensor(x_bias[w][:, i % 2, :, :], xs[2 * layer + w][:, b * NT:(b + 1) * NT, :],
                                   bias.unsqueeze(1).to_broadcast([P, NT, D]), ALU.add).then_inc(x_bias_ready[w], 1)

            def split(i):
                buf = i % 2
                if i >= 2:
                    pool.wait_ge(parts_stored[i - 2], 16 * 2 * NG)
                if i < B:
                    pool.wait_ge(rest_ready, i + 1)
                else:
                    pool.wait_ge(rot_ready, 2 * (i - B + 1))
                    link(pool.tensor_tensor(qk_full[:], rot_a[:], rot_b[:], ALU.add))
                    link(pool.tensor_copy(parts[:, buf, 0:4:3, :], qk_full[:]))
                    link(pool.tensor_tensor(rest[:], qk_full[:], parts[:, buf, 0:4:3, :], ALU.subtract))
                link(pool.tensor_copy(parts[:, buf, 1:5:3, :], rest[:]))
                pool.tensor_tensor(parts[:, buf, 2:6:3, :], rest[:], parts[:, buf, 1:5:3, :], ALU.subtract)\
                    .then_inc(parts_ready, 1)

            def split_max(i):
                buf = i % 2
                pool.wait_ge(max_done, s_number(i + 1))
                if i >= 2:
                    filled(pool, "maxrows", i - 2)
                nm = neg_parts[:, buf]
                link(pool.tensor_scalar(neg_max[:], row_max[:, buf], -1.0, None, ALU.mult))
                for n in range(3):
                    for qb in range(NT):
                        ins = pool.tensor_copy(nm[:, qb, :, n, :], neg_max[:, qb])
                    if n == 2:
                        break
                    link(ins)
                    for qb in range(NT):
                        ins = pool.tensor_tensor(neg_max[:, qb], neg_max[:, qb], nm[:, qb, :, n, :], ALU.subtract)
                    link(ins)
                ins.then_inc(negs_ready, 1)

            def mask_probs(i, n, unit):
                gs, kb, parity = unit
                number = t_number(i, n)
                pool.wait_ge(exp_done, number + 1)
                v = probs[:, kb, 4 * gs[0] + parity:4 * gs[-1] + 4:2, kb * P:(kb + 1) * P]
                pool.affine_select(out=v, in_=v, pattern=[[0, 2 * len(gs)], [1, P]], compare_op=ALU.is_ge, fill=0.0,
                    base=0, channel_multiplier=-1).then_inc(masked, 1)

            setup0()
            for t in range(SLOTS):
                if t in T_UNITS and T_UNITS[t][0] < B:
                    i, unit = T_UNITS[t]
                    mask_probs(i, t - T_AT[i], unit)
                for step, i in PLAN[t]:
                    if step in ("stats1", "stats2"):
                        centre(int(step[-1]) - 1, i)
                    elif step == "gates1":
                        setup_gated()
                    elif step == "times":
                        setup1()
                    elif step == ("qk_rot" if i >= B else "qk"):
                        split(i)
                    elif step == "maxrows":
                        split_max(i)
                        add_bias(0, i)
                    elif step == "turn2":
                        add_bias(1, i)


def constants():
    half = HD // 2
    inv = (1.0 / 10000.0 ** (np.arange(0, HD, 2, dtype=np.float32) / np.float32(HD))).astype(np.float32)
    angle = (np.arange(T, dtype=np.float32)[:, None] * inv[None, :]).astype(np.float32)
    both = np.stack([np.cos(angle), np.sin(angle)]).astype(np.float32)
    d = (np.arange(P) // HALF) % HD
    rope = np.ascontiguousarray(both[:, :, d % half].transpose(2, 0, 1))
    ahead = np.arange(P)[None, :] > np.arange(P)[:, None]
    return {"ident": np.eye(P, dtype=np.float32), "mask": np.where(ahead, np.float32(MASKED), np.float32(0)),
            "rope": rope}


def kernel(**inputs):
    import concourse.bacc as _bacc
    from concourse.bass_utils import run_bass_kernel_spmd as _run

    nc = _bacc.Bacc("TRN2", target_bir_lowering=False, num_devices=1)
    arrays, a, c = {}, {}, {}
    for name, value in inputs.items():
        v = np.ascontiguousarray(value)
        arrays[f"in_{name}"] = v
        a[name] = nc.dram_tensor(f"in_{name}", v.shape, mybir.dt.from_np(v.dtype), kind="ExternalInput").ap()
    for name, v in constants().items():
        arrays[f"const_{name}"] = v
        c[name] = nc.dram_tensor(f"const_{name}", v.shape, mybir.dt.from_np(v.dtype), kind="ExternalInput").ap()
    out = nc.dram_tensor("out_0", (B, T, D), F32, kind="ExternalOutput").ap()
    build(nc, a, out, c)
    r = _run(nc, [arrays], core_ids=[0])
    return r.results[0]["out_0"]
```

```python
from contextlib import ExitStack

import numpy as np

import concourse.bass as bass
from concourse import mybir

ALU = mybir.AluOpType
ACT = mybir.ActivationFunctionType
F32 = mybir.dt.float32
BF16 = mybir.dt.bfloat16
AX_X = mybir.AxisListType.X

P = 128
B, T, D = 4, 256, 128
H, HD = 16, 8
NT = T // P
LAYERS = 2
ITEMS = LAYERS * B
FF = 512
FC = FF // P
EPS = 1e-5
SCALE = HD ** -0.5
MASKED = -1e30
HALF = H // 2
GROUPS_Q = (0, 0, 0, 1, 1, 1, 2)
GROUPS_K = (0, 1, 2, 0, 1, 2, 0)
NG = len(GROUPS_Q)
SROWS = NG * HD
MROWS = SROWS + 3
VW = 32

ROWS = [("cond_1024", 4), ("L0_cond_bada", 6), ("L0_cond_g1", 1), ("L0_cond_be1", 1),
        ("L0_cond_g2", 1), ("L0_cond_be2", 1), ("L0_cond_b1", 4), ("L1_cond_w_norm1", 1),
        ("L1_cond_w_norm2", 1), ("L1_cond_t1_b1", 1), ("L1_cond_t2_b1", 1),
        ("L1_cond_t1_b2", 2), ("L1_cond_t2_b2", 2), ("turned bq", 1), ("turned bk", 1),
        ("rotated bq", 1), ("rotated bk", 1)]
NROWS = sum(n for _, n in ROWS)
PACKS = {
    "early": [("ident", P), ("w_qk", 2 * D), ("w_v", D), ("w_ada", 6 * D)],
    "layer0": [("mask", P), ("w_proj", D), ("w_1", FF), ("w_2", FF)],
    "attn1": [("rope", 2 * T), ("w_qk", 2 * D), ("w_rot", 2 * D), ("t_w1", 2 * D), ("t_w2", 4 * D), ("w_v", D), ("w_o", D)],
    "mlp1": [("w_gate", FF), ("w_up", FF), ("w_down", FF)],
}
WIDE = ["gate of attention", "gate of MLP", "L0_cond_bproj", "L0_cond_b2", "L1_cond_bv", "L1_cond_bo"]
COL = {name: sum(n for _, n in ROWS[:k]) for k, (name, _) in enumerate(ROWS)}


def score_units(i):
    units = []
    for qb in range(NT):
        keys = (qb + 1) * P if i < B else T
        n = 512 // keys
        units += [(qb, p, s, n, keys) for s in range(0, HALF, n) for p in range(2)]
    return units


def prob_units(i):
    if i < B:
        return [u for g in (0, 2) for u in
                [((g + k,), 0, p) for k in range(2) for p in range(2)] + [((g, g + 1), 1, p) for p in range(2)]]
    return [((g,), kb, p) for g in range(4) for kb in range(NT) for p in range(2)]


PRE_AT = [2.5, 8, 15, 28, 57, 71.5, 84.5, 101.5]
S_AT = [10.5, 23, 34, 47, 65, 81, 97, 112]
T_AT = [30, 42, 54, 67, 87, 104, 119, 135]
STEPS = {
    "tensor": {"turn1": ("pre", 1.1), "qk": ("pre", 2.2), "qk_rot": ("pre", 2.3), "v": ("pre", 2.5),
               "max_turn": ("max", 1.4), "out_turn0": ("post", 0.4), "out_turn1": ("post", 1.4),
               "on_turn": ("post", 3.4), "proj": ("post", 4.4), "turn2": ("post", 6.4), "gate0": ("post", 8.2),
               "hidden0": ("post", 8.3), "hidden1": ("post", 8.4), "up0": ("post", 8.4), "gate1": ("post", 8.5),
               "up1": ("post", 8.6), "down": ("post", 10.4)},
    "scalar": {"affine1": ("pre", 1.2), "high": ("pre", 2.3), "copy_v": ("pre", 2.3), "move_max": ("max", 1.6),
               "copy_on": ("post", 3.4), "affine2": ("post", 6.2), "gelu0": ("post", 8.4), "gelu1": ("post", 8.5)},
    "vector": {"stats1": ("pre", 0), "centre1": ("pre", 1), "rotate0": ("pre", 2.3), "rotate1": ("pre", 2.4),
               "split": ("pre", 2.5), "add_bv": ("pre", 2.6), "normalise0": ("post", 0.5),
               "normalise1": ("post", 1.5), "add_attention": ("post", 4.5), "stats2": ("post", 4.6),
               "centre2": ("post", 5.6), "times_up0": ("post", 8.5), "times_up1": ("post", 8.6),
               "add_mlp": ("post", 12.5)},
    "gpsimd": {"root1": ("pre", 0.1), "set_ones": ("pre", 1.2), "split_max": ("max", 0.6), "add_bias1": ("max", 3.6),
               "root2": ("post", 4.7), "add_bias2": ("post", 5.8)},
    "sync": {"stack": ("pre", 1.1), "store": ("post", 12)},
}
ONLY = {"qk_rot": 1, "rotate0": 1, "rotate1": 1, "add_bv": 1, "copy_v": 0, "hidden0": 0, "hidden1": 0,
        "gate0": 1, "up0": 1, "gate1": 1, "up1": 1, "times_up0": 1, "times_up1": 1, "set_ones": 0,
        "add_bias2": 0, "store": 1}
SETUP = {
    "tensor": {"rows": -0.3, "mods": 0.1, "gates0": 3.2, "gates1": 3.3, "times": 8.2, "times2": 9.2},
    "scalar": {"rows": 0, "times": 5.3},
    "vector": {"rows": -0.2, "mods": -0.1, "gates0": 3.2, "gates1": 3.3, "times": 8.2, "times2": 9.2},
    "gpsimd": {"start": -1, "cast_mask": 2.5, "gated": 3.3},
    "sync": {"loads": -1, "late_loads": 2.8},
}
PV_LAG = 2.2
SCORES, MAXIMA, SCORES_T = 0.4, 0.9, 0


def programs():
    out = {engine: [(t, step, 0, 0) for step, t in steps.items()] for engine, steps in SETUP.items()}
    for i in range(ITEMS):
        s_units, t_units = score_units(i), prob_units(i)
        for n in range(len(s_units)):
            out["tensor"].append((S_AT[i] + n + SCORES, "scores", i, n))
            out["vector"].append((S_AT[i] + n + MAXIMA, "maxima", i, n))
        pv_at = {}
        for n, (groups, kb, _) in enumerate(t_units):
            out["tensor"].append((T_AT[i] + n + SCORES_T, "scores_t", i, n))
            out["scalar"].append((T_AT[i] + n, "exp", i, n))
            if i < B:
                out["gpsimd"].append((T_AT[i] + n, "mask_probs", i, n))
            for g in groups:
                for k in (0, 1) if i < B and kb else (kb,):
                    pv_at[g, k] = T_AT[i] + n + PV_LAG + (g % 2 if i < B else 0) + 0.01 * k
        for (g, kb), t in pv_at.items():
            out["tensor"].append((t, "pv", i, (g, kb)))
            if g % 2 and kb:
                out["scalar"].append((t + 0.05, "copy_o", i, g // 2))
        base = {"pre": PRE_AT[i], "max": S_AT[i] + len(s_units), "post": max(pv_at.values()) - 0.2}
        for engine, steps in STEPS.items():
            out[engine] += [(base[b] + t, step, i, 0) for step, (b, t) in steps.items() if ONLY.get(step, i // B) == i // B]
    return {engine: sorted(steps, key=lambda x: x[0]) for engine, steps in out.items()}


PROGRAMS = programs()

M_BANKS = 3
USE = {(step, i): n for n, (step, i) in enumerate(
    (step, i) for _, step, i, _ in PROGRAMS["tensor"] if step not in ("scores", "scores_t", "pv"))}
BANK_STEPS = list(USE)


def s_number(i, n=0):
    return sum(len(score_units(j)) for j in range(i)) + n


def t_number(i, n=0):
    return sum(len(prob_units(j)) for j in range(i)) + n


def t_done(i, g, kb):
    return t_number(i) + max(n + 1 for n, u in enumerate(prob_units(i)) if g in u[0] and u[1] == kb)


def pv_number(i, g, kb):
    return (i * 4 + g) * NT + kb


def build(nc, a, out):
    with ExitStack() as ctx:
        def sb(name, shape, dt=F32):
            return ctx.enter_context(nc.sbuf_tensor(name, shape, dt))

        def sem(name):
            return ctx.enter_context(nc.semaphore(name))

        banks = [ctx.enter_context(nc.psum_tensor(f"bank{k}", [P, 512], F32)) for k in range(8)]
        s_bank, t_bank, o_bank, m_bank = banks[0:2], banks[2:4], banks[4], banks[5:5 + M_BANKS]

        packs = {name: sb(f"pack_{name}", [P, sum(n for _, n in held)]) for name, held in PACKS.items()}

        def packed(pack, name):
            at = 0
            for held, n in PACKS[pack]:
                if held == name:
                    return packs[pack][:, at:at + n]
                at += n

        ident = packed("early", "ident")
        w_ada = packed("early", "w_ada").rearrange("p (k d) -> p k d", k=6)
        w_qk = [packed(name, "w_qk").rearrange("p (k d) -> p k d", k=2) for name in ("early", "attn1")]
        w_v = [packed(name, "w_v") for name in ("early", "attn1")]
        mask = packed("layer0", "mask")
        w_proj = packed("layer0", "w_proj")
        w_1 = packed("layer0", "w_1")
        w_2 = packed("layer0", "w_2").rearrange("p (c d) -> p c d", c=FC)
        rope = packed("attn1", "rope").rearrange("p (k t) -> p k t", k=2)
        w_rot = packed("attn1", "w_rot").rearrange("p (k d) -> p k d", k=2)
        t_w1 = packed("attn1", "t_w1").rearrange("p (k d) -> p k d", k=2)
        t_w2 = packed("attn1", "t_w2").rearrange("p (k n d) -> p k n d", k=2, n=2)
        w_o = packed("attn1", "w_o")
        w_gate = packed("mlp1", "w_gate")
        w_up = packed("mlp1", "w_up")
        w_down = packed("mlp1", "w_down").rearrange("p (c d) -> p c d", c=FC)
        rows = sb("rows", [NROWS, P])
        cols = sb("cols", [P, NROWS])
        wide = sb("wide", [P, len(WIDE), D])
        bproj_row, b2_row, bv_row, bo_row = (wide[:, k, :] for k in range(2, 6))
        ident_bf = sb("ident_bf", [P, P], BF16)
        mask_bf = sb("mask_bf", [P, P], BF16)
        silu = sb("silu", [P, 4, B])
        silu_wide = sb("silu_wide", [P, B, P])
        mod = sb("mod", [P, 4, B])
        gates = sb("gates", [P, 2, B, D])
        tsilu = sb("tsilu", [P, 5, 2, B])
        tmod = sb("tmod", [P, 2, 2, B])
        mul_c = sb("mul_c", [P, LAYERS, 2, B])
        add_c = sb("add_c", [P, LAYERS, 2, B])
        w_projg = sb("w_projg", [P, B, D])
        w_2g = sb("w_2g", [P, B, FC, D])
        add_attn = sb("add_attn", [P, B, D])
        add_mlp = sb("add_mlp", [P, B, D])
        xs = [sb(f"x{k}", [P, B * NT, D]) for k in range(2 * LAYERS)]
        xs.append(xs[0])
        bn = sb("bn", [P, 2, NT, 6])
        mean_var = sb("mean_var", [P, 2, 2, NT, 2])
        var_eps = sb("var_eps", [P, 2, 2, NT])
        rstd = sb("rstd", [P, 2, 2, NT])
        minus_half = sb("minus_half", [P, NT])
        square = sb("square", [P, NT])
        xn = [sb(f"xn{w}", [P, 2, NT, D]) for w in range(2)]
        x_bias = [sb(f"x_bias{w}", [P, 2, NT, D]) for w in range(2)]
        xmt = [sb(f"xmt{w}", [P, 2, T]) for w in range(2)]
        rot_a = sb("rot_a", [P, 2, T])
        rot_b = sb("rot_b", [P, 2, T])
        qk_full = sb("qk_full", [P, 2, T])
        rest = sb("rest", [P, 2, T])
        parts = sb("parts", [P, 2, 2 * NG, T], BF16)
        stacks = sb("stacks", [P, B, 2, HALF, T], BF16)
        v_sb = sb("v_sb", [P, B * NT, H, VW])
        row_max = sb("row_max", [P, 2, NT, 2, HALF])
        max_rest = sb("max_rest", [P, 2, NT, 2, HALF])
        max_parts = sb("max_parts", [P, 2, NT, 2, 3, HALF], BF16)
        max_rows = sb("max_rows", [2 * 3 * HALF, 2, T], BF16)
        probs = sb("probs", [P, NT, H, T])
        o_t = sb("o_t", [P, 2, 4, T])
        denom = sb("denom", [P, NT, H])
        o_n = sb("o_n", [P, 2, NT, D])
        o_nt = sb("o_nt", [P, 2, T])
        gelu = sb("gelu", [P, 2, 2, T])
        hidden = sb("hidden", [P, 2, FC, T])
        scratch = nc.dram_tensor("stack_scratch", (2, 2, 2 * NG, 64, T), BF16, kind="Internal").ap()

        x_loaded = [sem(f"x_loaded{b}") for b in range(B)]
        rows_loaded = sem("rows_loaded")
        loaded = {name: sem(f"{name}_loaded") for name in PACKS}
        wide_loaded = sem("wide_loaded")
        casts_ready = sem("casts_ready")
        minus_ones = sem("minus_ones")
        v_ones = sem("v_ones")
        cols_ready = sem("cols_ready")
        neg_exp = sem("neg_exp")
        silu_ready = sem("silu_ready")
        norm0_ready = sem("norm0_ready")
        norm1_ready = sem("norm1_ready")
        wide_ready = sem("wide_ready")
        gates_ready = sem("gates_ready")
        gated_ready = sem("gated_ready")
        tz_ready = sem("tz_ready")
        texp_ready = sem("texp_ready")
        tsilu_ready = sem("tsilu_ready")
        vchain = sem("vchain")
        pchain = sem("pchain")
        stats_ready = [sem(f"stats_ready{w}") for w in range(2)]
        rstd_ready = [sem(f"rstd_ready{w}") for w in range(2)]
        xn_ready = [sem(f"xn_ready{w}") for w in range(2)]
        x_bias_ready = [sem(f"x_bias_ready{w}") for w in range(2)]
        xmt_ready = [sem(f"xmt_ready{w}") for w in range(2)]
        bank_filled = sem("bank_filled")
        high_ready = sem("high_ready")
        rest_ready = sem("rest_ready")
        full_ready = sem("full_ready")
        rot_ready = sem("rot_ready")
        parts_ready = sem("parts_ready")
        parts_stored = [sem(f"parts_stored{i}") for i in range(ITEMS)]
        stacks_loaded = [sem(f"stacks_loaded{i}") for i in range(ITEMS)]
        v_ready = sem("v_ready")
        s_filled = sem("s_filled")
        max_done = sem("max_done")
        max_split = sem("max_split")
        max_rows_ready = sem("max_rows_ready")
        max_rows_placed = [sem(f"max_rows_placed{i}") for i in range(ITEMS)]
        t_filled = sem("t_filled")
        exp_done = sem("exp_done")
        masked = sem("masked")
        pv_done = sem("pv_done")
        o_copied = sem("o_copied")
        on_ready = sem("on_ready")
        ont_ready = sem("ont_ready")
        mid_ready = sem("mid_ready")
        gelu_ready = sem("gelu_ready")
        hidden_ready = sem("hidden_ready")
        end_ready = sem("end_ready")
        out_stored = sem("out_stored")

        block = ctx.enter_context(nc.Block())

        def bank_of(step, i):
            return m_bank[USE[step, i] % M_BANKS]

        def filled(eng, step, i):
            eng.wait_ge(bank_filled, USE[step, i] + 1)

        def col(name, k=0):
            return cols[:, COL[name] + k:COL[name] + k + 1]

        @block.sync
        def _(sp):
            def load(dst, name, signal):
                sp.dma_start(dst, a[name] if isinstance(name, str) else name).then_inc(signal, 16)

            def load_x(b):
                load(xs[0][:, b * NT:(b + 1) * NT, :], a["x"][b].rearrange("(j p) d -> p j d", p=P), x_loaded[b])

            def first_loads():
                load(rows[:], "rows", rows_loaded)
                load(packs["early"][:], "early", loaded["early"])
                for b in range(2):
                    load_x(b)
                load(wide[:].rearrange("p k d -> p (k d)"), a["wide"].partition_broadcast(P), wide_loaded)
                load(packs["layer0"][:], "layer0", loaded["layer0"])
                for b in range(2, B):
                    load_x(b)

            def make_stacks(i):
                b, buf = i % B, i % 2
                sp.wait_ge(parts_ready, i + 1)
                if i >= 2:
                    sp.wait_ge(stacks_loaded[i - 2], 32)
                for p in range(2):
                    sp.dma_start(scratch[buf, p].rearrange("g r t -> r g t"),
                                 parts[64 * p:64 * p + 64, buf, :, :]).then_inc(parts_stored[i], 16)
                sp.wait_ge(parts_stored[i], 32)
                if i < B:
                    sp.wait_ge(minus_ones, i + 1)
                if i >= B:
                    sp.wait_ge(s_filled, s_number(i - B + 1))
                    sp.wait_ge(t_filled, t_number(i - B + 1))
                for p in range(2):
                    sp.dma_start(
                        stacks[64 * p:64 * p + SROWS, b, :, :, :].rearrange("r k s t -> r k (s t)"),
                        scratch[buf, p].rearrange("(k g) (d s) t -> (g d) k (s t)", k=2, s=HALF),
                    ).then_inc(stacks_loaded[i], 16)

            for _, step, i, _ in PROGRAMS["sync"]:
                if step == "loads":
                    first_loads()
                elif step == "stack":
                    make_stacks(i)
                elif step == "late_loads":
                    for name in ("attn1", "mlp1"):
                        load(packs[name][:], name, loaded[name])
                elif step == "store":
                    b = i % B
                    sp.wait_ge(end_ready, i + 1)
                    sp.dma_start(out[b].rearrange("(j p) d -> p j d", p=P),
                                 xs[4][:, b * NT:(b + 1) * NT, :]).then_inc(out_stored, 16)
            sp.wait_ge(out_stored, 16 * B)

        @block.tensor
        def _(pe):
            def reader_of(step, i):
                k = int(step[-1]) if step[-1].isdigit() else 0
                if step in ("turn1", "turn2"):
                    return xmt_ready[k - 1], i + 1
                return {
                    "rows": (cols_ready, 1), "mods": (norm0_ready, 1), "gates": (gates_ready, k + 1),
                    "times": (norm1_ready if k else tz_ready, 1),
                    "qk": (rot_ready, 2 * (i - B) + 1) if i >= B else (rest_ready, i + 1),
                    "qk_rot": (rot_ready, 2 * (i - B) + 2), "v": (v_ready, i + 1),
                    "max_turn": (max_rows_ready, i + 1), "out_turn": (on_ready, NT * i + k + 1),
                    "on_turn": (ont_ready, i + 1), "proj": (mid_ready, i + 1),
                    "hidden": (hidden_ready, 2 * i + k + 1), "gate": (gelu_ready, 2 * (i - B) + k + 1),
                    "up": (hidden_ready, 2 * i + k + 1), "down": (end_ready, i + 1),
                }[step.rstrip("012")]

            def take_bank(step, i):
                n = USE[step, i]
                if n >= M_BANKS:
                    pe.wait_ge(*reader_of(*BANK_STEPS[n - M_BANKS]))
                return m_bank[n % M_BANKS]

            def mm(o, lhs, rhs, start=True, stop=True):
                return pe.matmul(o, lhs, rhs, start=start, stop=stop)

            def rows_to_cols():
                bank = take_bank("rows", 0)
                pe.wait_ge(rows_loaded, 16)
                pe.wait_ge(loaded["early"], 16)
                pe.transpose(bank[:, 0:NROWS], rows[:], ident[0:NROWS, 0:NROWS]).then_inc(bank_filled, 1)

            def mods():
                bank = take_bank("mods", 0)
                pe.wait_ge(silu_ready, 1)
                for n, chunk in enumerate((0, 1, 3, 4)):
                    last = mm(bank[:, n * B:(n + 1) * B], w_ada[:, chunk, :], silu[:, 3, :])
                last.then_inc(bank_filled, 1)

            def gate_rows(k):
                bank = take_bank(f"gates{k}", 0)
                pe.wait_ge(wide_ready, 1)
                for b in range(B):
                    last = mm(bank[:, b * D:(b + 1) * D], silu_wide[:, b, :], w_ada[:, 2 + 3 * k, :])
                last.then_inc(bank_filled, 1)

            def times():
                bank = take_bank("times", 0)
                pe.wait_ge(loaded["attn1"], 16)
                for k in range(2):
                    last = mm(bank[:, k * B:(k + 1) * B], t_w1[:, k, :], cols[:, 0:B])
                last.then_inc(bank_filled, 1)

            def times2():
                bank = take_bank("times2", 0)
                pe.wait_ge(tsilu_ready, 1)
                for k in range(2):
                    for n in range(2):
                        last = mm(bank[:, (2 * k + n) * B:(2 * k + n + 1) * B], t_w2[:, k, n, :], tsilu[:, 4, k, :])
                last.then_inc(bank_filled, 1)

            def turn(w, i):
                bank = take_bank(f"turn{w + 1}", i)
                for j in range(NT):
                    pe.wait_ge(xn_ready[w], NT * i + j + 1)
                    last = pe.transpose(bank[:, j * P:(j + 1) * P], xn[w][:, i % 2, j, :], ident)
                last.then_inc(bank_filled, 1)

            def project_qk(i, rotated=False):
                layer = i // B
                bank = take_bank("qk_rot" if rotated else "qk", i)
                pe.wait_ge(xmt_ready[0], i + 1)
                for k in range(2):
                    w = w_rot[:, k, :] if rotated else w_qk[layer][:, k, :]
                    last = mm(bank[:, k * T:(k + 1) * T], w, xmt[0][:, i % 2, :])
                last.then_inc(bank_filled, 1)

            def project_v(i):
                bank = take_bank("v", i)
                for j in range(NT):
                    last = mm(bank[:, j * D:(j + 1) * D], xmt[0][:, i % 2, j * P:(j + 1) * P], w_v[i // B])
                last.then_inc(bank_filled, 1)

            def scores(i, n, unit):
                qb, p, s0, heads, keys = unit
                b, number = i % B, s_number(i, n)
                bank = s_bank[number % 2]
                if n == 0:
                    pe.wait_ge(stacks_loaded[i], 32)
                if number == 0:
                    pe.wait_ge(casts_ready, 2)
                if number >= 2:
                    pe.wait_ge(max_done, number - 1)
                r = slice(64 * p, 64 * p + SROWS)
                for k in range(heads):
                    o = bank[:, k * keys:(k + 1) * keys]
                    last = mm(o, stacks[r, b, 0, s0 + k, qb * P:(qb + 1) * P], stacks[r, b, 1, s0 + k, 0:keys],
                              stop=i >= B)
                    if i < B:
                        last = mm(o[:, keys - P:keys], ident_bf[:], mask_bf[:], start=False)
                last.then_inc(s_filled, 1)

            def place_max(i):
                bank = take_bank("max_turn", i)[:].bitcast(BF16)
                pe.wait_ge(max_split, i + 1)
                for qb in range(NT):
                    last = pe.transpose(bank[0:48, qb * P:(qb + 1) * P],
                                        max_parts[:, i % 2, qb].rearrange("q p n s -> q (p n s)"), ident_bf[:])
                last.then_inc(bank_filled, 1)

            def scores_t(i, n, unit):
                gs, kb, parity = unit
                b, number = i % B, t_number(i, n)
                bank = t_bank[number % 2]
                if n == 0:
                    pe.wait_ge(max_rows_placed[i], 16 * 6)
                if number >= 2:
                    pe.wait_ge(exp_done, number - 1)
                q0 = (len(gs) - 1) * P
                for k, (g, j) in enumerate((g, j) for g in gs for j in (parity, parity + 2)):
                    p, s = j % 2, 2 * g + j // 2
                    r = slice(64 * p, 64 * p + MROWS)
                    last = mm(bank[:, k * (T - q0):(k + 1) * (T - q0)],
                              stacks[r, b, 1, s, kb * P:(kb + 1) * P], stacks[r, b, 0, s, q0:T])
                last.then_inc(t_filled, 1)

            def pv(i, g, kb):
                b = i % B
                if g == 0 and kb == 0:
                    pe.wait_ge(v_ready, i + 1)
                if g % 2 == 0 and kb == 0 and 2 * i + g // 2 >= 1:
                    pe.wait_ge(o_copied, 2 * i + g // 2)
                if i < B:
                    pe.wait_ge(masked, t_done(i, g, kb))
                else:
                    pe.wait_ge(exp_done, t_done(i, g, kb))
                q0 = P if i < B and kb == 1 else 0
                bank = o_bank
                for j in range(4):
                    last = pe.matmul(bank[32 * j:32 * j + VW, (g % 2) * T + q0:(g % 2 + 1) * T],
                                     v_sb[:, b * NT + kb, 4 * g + j, :], probs[:, kb, 4 * g + j, q0:T],
                                     start=(kb == 0), stop=(kb == NT - 1), tile_position=(0, 32 * j))
                last.then_inc(pv_done, 1)

            def out_turn(i, qb):
                bank = take_bank(f"out_turn{qb}", i)
                pe.wait_ge(o_copied, 2 * (i + 1))
                for g in range(4):
                    last = pe.transpose(bank[:, g * P:(g + 1) * P], o_t[:, i % 2, g, qb * P:(qb + 1) * P], ident)
                last.then_inc(bank_filled, 1)

            def turn_out(i):
                bank = take_bank("on_turn", i)
                for j in range(NT):
                    pe.wait_ge(on_ready, NT * i + j + 1)
                    last = pe.transpose(bank[:, j * P:(j + 1) * P], o_n[:, i % 2, j, :], ident)
                last.then_inc(bank_filled, 1)

            def project_out(i):
                bank = take_bank("proj", i)
                if i == 0:
                    pe.wait_ge(gated_ready, 1)
                pe.wait_ge(ont_ready, i + 1)
                w = w_o if i >= B else w_projg[:, i % B, :]
                for j in range(NT):
                    last = mm(bank[:, j * D:(j + 1) * D], o_nt[:, i % 2, j * P:(j + 1) * P], w)
                last.then_inc(bank_filled, 1)

            def mlp_in(step, i, w):
                half = int(step[-1])
                bank = take_bank(step, i)
                pe.wait_ge(xmt_ready[1], i + 1)
                if i == B:
                    pe.wait_ge(loaded["mlp1"], 16)
                for k in range(2):
                    c = 2 * half + k
                    last = mm(bank[:, k * T:(k + 1) * T], w[:, c * P:(c + 1) * P], xmt[1][:, i % 2, :])
                last.then_inc(bank_filled, 1)

            def mlp_out(i):
                bank = take_bank("down", i)
                if i == 0:
                    pe.wait_ge(gated_ready, 2)
                pe.wait_ge(hidden_ready, 2 * (i + 1))
                for j in range(NT):
                    for c in range(FC):
                        w = w_down[:, c, :] if i >= B else w_2g[:, i % B, c, :]
                        last = mm(bank[:, j * D:(j + 1) * D], hidden[:, i % 2, c, j * P:(j + 1) * P], w,
                                  start=(c == 0), stop=(c == FC - 1))
                last.then_inc(bank_filled, 1)

            for _, step, i, n in PROGRAMS["tensor"]:
                if step == "scores_t":
                    scores_t(i, n, prob_units(i)[n])
                elif step == "pv":
                    pv(i, *n)
                elif step == "scores":
                    scores(i, n, score_units(i)[n])
                elif step == "rows":
                    rows_to_cols()
                elif step == "mods":
                    mods()
                elif step in ("gates0", "gates1"):
                    gate_rows(int(step[-1]))
                elif step == "times":
                    times()
                elif step == "times2":
                    times2()
                elif step in ("turn1", "turn2"):
                    turn(int(step[-1]) - 1, i)
                elif step == "qk":
                    project_qk(i)
                elif step == "qk_rot":
                    project_qk(i, rotated=True)
                elif step == "v":
                    project_v(i)
                elif step == "max_turn":
                    place_max(i)
                elif step in ("out_turn0", "out_turn1"):
                    out_turn(i, int(step[-1]))
                elif step == "on_turn":
                    turn_out(i)
                elif step == "proj":
                    project_out(i)
                elif step in ("hidden0", "hidden1"):
                    mlp_in(step, i, w_1)
                elif step in ("gate0", "gate1"):
                    mlp_in(step, i, w_gate)
                elif step in ("up0", "up1"):
                    mlp_in(step, i, w_up)
                elif step == "down":
                    mlp_out(i)

        @block.scalar
        def _(act):
            def affine(w, i):
                layer, b = divmod(i, B)
                step = f"turn{w + 1}"
                if i == 0 and w == 0:
                    act.wait_ge(norm0_ready, 1)
                if i == B and w == 0:
                    act.wait_ge(norm1_ready, 1)
                if i >= 2:
                    filled(act, ("v" if w == 0 else "hidden1" if i - 2 < B else "up1"), i - 2)
                filled(act, step, i)
                ins = act.activation(xmt[w][:, i % 2, :], bank_of(step, i)[:, 0:T], ACT.Identity,
                                     bias=add_c[:, layer, w, b:b + 1], scale=mul_c[:, layer, w, b:b + 1])
                ins.then_inc(xmt_ready[w], 1)

            def high_part(i):
                if i >= 2:
                    act.wait_ge(parts_stored[i - 2], 32)
                filled(act, "qk", i)
                act.activation(parts[:, i % 2, 0:NG + 1:NG, :], bank_of("qk", i)[:].rearrange("c (k t) -> c k t", k=2),
                               ACT.Copy).then_inc(high_ready, 1)

            def high_part1(i):
                act.wait_ge(full_ready, i - B + 1)
                act.wait_ge(parts_stored[i - 2], 32)
                act.activation(parts[:, i % 2, 0:NG + 1:NG, :], qk_full[:], ACT.Copy).then_inc(high_ready, 1)

            def copy_v(i):
                b = i % B
                act.wait_ge(v_ones, i + 1)
                filled(act, "v", i)
                ins = act.activation(v_sb[:, b * NT:(b + 1) * NT, :, 0:HD],
                                     bank_of("v", i)[:, 0:T].rearrange("k (j h d) -> k j h d", j=NT, h=H), ACT.Copy)
                ins.then_inc(v_ready, 1)

            def move_max(i):
                b = i % B
                if i >= 2:
                    act.wait_ge(max_rows_placed[i - 2], 16 * 6)
                filled(act, "max_turn", i)
                ins = act.activation(max_rows[:, i % 2, :], bank_of("max_turn", i)[:].bitcast(BF16)[0:48, 0:T], ACT.Copy)
                ins.then_inc(max_rows_ready, 1)
                act.wait_ge(max_rows_ready, i + 1)
                for p in range(2):
                    for n in range(3):
                        r = (p * 3 + n) * HALF
                        row = 64 * p + SROWS + n
                        act.dma_start(stacks[row:row + 1, b, 0, :, :],
                                      max_rows[r:r + HALF, i % 2, :]).then_inc(max_rows_placed[i], 16)

            def exponentials(i, n, unit):
                gs, kb, parity = unit
                if i >= 1:
                    act.wait_ge(pv_done, pv_number(i, gs[-1], kb) - 4 * NT + 1)
                number = t_number(i, n)
                act.wait_ge(t_filled, number + 1)
                q0 = (len(gs) - 1) * P
                dst = probs[:, kb, 4 * gs[0] + parity:4 * gs[-1] + 4:2, q0:T]
                src = t_bank[number % 2][:].rearrange("k (h q) -> k h q", h=2 * len(gs))
                act.activation(dst, src, ACT.Exp, scale=SCALE).then_inc(exp_done, 1)

            def copy_o(i, pair):
                if i >= 2:
                    filled(act, "out_turn1", i - 2)
                act.wait_ge(pv_done, pv_number(i, 2 * pair + 1, 1) + 1)
                act.activation(o_t[:, i % 2, 2 * pair:2 * pair + 2, :],
                               o_bank[:].rearrange("r (g q) -> r g q", g=2), ACT.Copy).then_inc(o_copied, 1)

            def copy_ont(i):
                if i >= 2:
                    filled(act, "proj", i - 2)
                filled(act, "on_turn", i)
                ins = act.activation(o_nt[:, i % 2, :], bank_of("on_turn", i)[:, 0:T], ACT.Copy)
                ins.then_inc(ont_ready, 1)

            def hidden_gelu(half, i):
                step = f"hidden{half}"
                if i >= 2 and half == 0:
                    filled(act, "down", i - 2)
                filled(act, step, i)
                for k in range(2):
                    c = 2 * half + k
                    ins = act.activation(hidden[:, i % 2, c, :], bank_of(step, i)[:, k * T:(k + 1) * T],
                                         ACT.Gelu, bias=col("L0_cond_b1", c))
                ins.then_inc(hidden_ready, 1)

            def gate_gelu(half, i):
                step = f"gate{half}"
                if 2 * (i - B) + half >= 2:
                    act.wait_ge(hidden_ready, 2 * i + half - 1)
                filled(act, step, i)
                act.activation(gelu[:, half, :, :], bank_of(step, i)[:].rearrange("f (k t) -> f k t", k=2),
                               ACT.Gelu).then_inc(gelu_ready, 1)

            for _, step, i, n in PROGRAMS["scalar"]:
                if step == "exp":
                    exponentials(i, n, prob_units(i)[n])
                elif step == "copy_o":
                    copy_o(i, n)
                elif step == "rows":
                    act.wait_ge(cols_ready, 1)
                    act.activation(silu[:, 0, :], cols[:, 0:B], ACT.Exp, scale=-1.0).then_inc(neg_exp, 1)
                elif step == "times":
                    act.wait_ge(tz_ready, 1)
                    act.activation(tsilu[:, 1, :, :], tsilu[:, 0, :, :], ACT.Exp, scale=-1.0).then_inc(texp_ready, 1)
                elif step in ("affine1", "affine2"):
                    affine(int(step[-1]) - 1, i)
                elif step == "high":
                    high_part(i) if i < B else high_part1(i)
                elif step == "copy_v":
                    copy_v(i)
                elif step == "move_max":
                    move_max(i)
                elif step == "copy_on":
                    copy_ont(i)
                elif step in ("gelu0", "gelu1"):
                    gelu_half = int(step[-1])
                    hidden_gelu(gelu_half, i) if i < B else gate_gelu(gelu_half, i)

        @block.vector
        def _(dve):
            links = [0]

            def link(ins):
                links[0] += 1
                ins.then_inc(vchain, 1)
                dve.wait_ge(vchain, links[0])

            def cond_silu():
                filled(dve, "rows", 0)
                dve.tensor_copy(cols[:], bank_of("rows", 0)[:, 0:NROWS]).then_inc(cols_ready, 1)
                dve.wait_ge(neg_exp, 1)
                link(dve.tensor_scalar_add(silu[:, 1, :], silu[:, 0, :], 1.0))
                link(dve.reciprocal(silu[:, 2, :], silu[:, 1, :]))
                dve.tensor_tensor(silu[:, 3, :], silu[:, 2, :], cols[:, 0:B], ALU.mult).then_inc(silu_ready, 1)
                dve.wait_ge(silu_ready, 1)
                dve.tensor_copy(silu_wide[:], silu[:, 3, :].unsqueeze(2).to_broadcast([P, B, P])).then_inc(wide_ready, 1)

            def norm_mods():
                filled(dve, "mods", 0)
                for n, chunk in enumerate((0, 1, 3, 4)):
                    ins = dve.tensor_scalar(mod[:, n, :], bank_of("mods", 0)[:, n * B:(n + 1) * B],
                                            col("L0_cond_bada", chunk), float(n % 2), ALU.add, ALU.add)
                link(ins)
                for w in range(2):
                    dve.tensor_scalar(mul_c[:, 0, w, :], mod[:, 2 * w + 1, :], col(f"L0_cond_g{w + 1}"), None, ALU.mult)
                    ins = dve.scalar_tensor_tensor(add_c[:, 0, w, :], mod[:, 2 * w + 1, :], col(f"L0_cond_be{w + 1}"),
                                                   mod[:, 2 * w, :], ALU.mult, ALU.add)
                ins.then_inc(norm0_ready, 1)

            def gate_rows(k):
                step = f"gates{k}"
                if k == 0:
                    dve.wait_ge(wide_loaded, 16)
                filled(dve, step, 0)
                dve.tensor_tensor(gates[:, k, :, :], bank_of(step, 0)[:].rearrange("p (b d) -> p b d", b=B),
                                  wide[:, k, :].unsqueeze(1).to_broadcast([P, B, D]), ALU.add).then_inc(gates_ready, 1)

            def times():
                filled(dve, "times", 0)
                bank = bank_of("times", 0)
                for k in range(2):
                    ins = dve.tensor_scalar(tsilu[:, 0, k, :], bank[:, k * B:(k + 1) * B], col(f"L1_cond_t{k + 1}_b1"),
                                            None, ALU.add)
                ins.then_inc(tz_ready, 1)
                dve.wait_ge(texp_ready, 1)
                link(dve.tensor_scalar_add(tsilu[:, 2, :, :], tsilu[:, 1, :, :], 1.0))
                link(dve.reciprocal(tsilu[:, 3, :, :], tsilu[:, 2, :, :]))
                dve.tensor_tensor(tsilu[:, 4, :, :], tsilu[:, 3, :, :], tsilu[:, 0, :, :], ALU.mult).then_inc(tsilu_ready, 1)

            def times2():
                filled(dve, "times2", 0)
                bank = bank_of("times2", 0)
                for k in range(2):
                    ins = dve.tensor_scalar(tmod[:, k, 0, :], bank[:, 2 * k * B:(2 * k + 1) * B],
                                            col(f"L1_cond_t{k + 1}_b2", 0), 1.0, ALU.add, ALU.add)
                    dve.tensor_scalar(add_c[:, 1, k, :], bank[:, (2 * k + 1) * B:(2 * k + 2) * B],
                                      col(f"L1_cond_t{k + 1}_b2", 1), None, ALU.add)
                link(ins)
                for k in range(2):
                    ins = dve.tensor_scalar(mul_c[:, 1, k, :], tmod[:, k, 0, :], col(f"L1_cond_w_norm{k + 1}"),
                                            None, ALU.mult)
                ins.then_inc(norm1_ready, 1)

            def stats(w, i):
                layer, b = divmod(i, B)
                if w == 0:
                    if layer == 0:
                        dve.wait_ge(x_loaded[b], 16)
                    else:
                        dve.wait_ge(end_ready, i - B + 1)
                else:
                    dve.wait_ge(mid_ready, i + 1)
                if i >= 2:
                    dve.wait_ge(rstd_ready[w], i - 1)
                x = xs[2 * layer + w]
                for j in range(NT):
                    ins = dve.bn_stats(bn[:, w, j, :], x[:, b * NT + j, :])
                link(ins)
                mv = mean_var[:, w, i % 2]
                for j in range(NT):
                    ins = dve.bn_aggr(mv[:, j, :], bn[:, w, j, :])
                link(ins)
                if layer:
                    link(dve.tensor_tensor(square[:], mv[:, :, 0], mv[:, :, 0], ALU.mult))
                    ins = dve.scalar_tensor_tensor(var_eps[:, w, i % 2, :], square[:], EPS, mv[:, :, 1], ALU.add, ALU.add)
                else:
                    ins = dve.tensor_scalar_add(var_eps[:, w, i % 2, :], mv[:, :, 1], EPS)
                ins.then_inc(stats_ready[w], 1)

            def centre(w, i):
                layer, b = divmod(i, B)
                x = xs[2 * layer + w]
                if i >= 2:
                    filled(dve, f"turn{w + 1}", i - 2)
                dve.wait_ge(rstd_ready[w], i + 1)
                for j in range(NT):
                    scale = rstd[:, w, i % 2, j:j + 1]
                    if layer == 0:
                        ins = dve.tensor_scalar(xn[w][:, i % 2, j, :], x[:, b * NT + j, :],
                                                mean_var[:, w, i % 2, j, 0:1], scale, ALU.subtract, ALU.mult)
                    else:
                        ins = dve.tensor_scalar(xn[w][:, i % 2, j, :], x[:, b * NT + j, :], scale, None, ALU.mult)
                    ins.then_inc(xn_ready[w], 1)

            def split(i):
                pt = parts[:, i % 2]
                high, middle, low = pt[:, 0:NG + 1:NG, :], pt[:, 3:NG + 2:NG - 2, :], pt[:, 6:NG + 3:NG - 4, :]
                if i < B:
                    full = bank_of("qk", i)[:].rearrange("c (k t) -> c k t", k=2)
                else:
                    full = qk_full[:]
                dve.wait_ge(high_ready, i + 1)
                ins = dve.tensor_tensor(rest[:], full, high, ALU.subtract)
                ins.then_inc(rest_ready, 1)
                dve.wait_ge(rest_ready, i + 1)
                link(dve.tensor_copy(middle, rest[:]))
                link(dve.tensor_tensor(low, rest[:], middle, ALU.subtract))
                dve.tensor_copy(pt[:, 1:3, :], pt[:, 0:1, :].to_broadcast([P, 2, T]))
                dve.tensor_copy(pt[:, 4:6, :], pt[:, 3:4, :].to_broadcast([P, 2, T]))
                dve.tensor_copy(pt[:, NG + 3:NG + 6, :], pt[:, NG:NG + 3, :])
                dve.tensor_copy(pt[:, NG + 6, :], pt[:, NG, :]).then_inc(parts_ready, 1)

            def rotate(i, sines):
                step = "qk_rot" if sines else "qk"
                filled(dve, step, i)
                dst = rot_b if sines else rot_a
                for k in range(2):
                    ins = dve.scalar_tensor_tensor(dst[:, k, :], bank_of(step, i)[:, k * T:(k + 1) * T],
                                                   col("rotated bq" if sines else "turned bq", k), rope[:, int(sines), :], ALU.add, ALU.mult)
                ins.then_inc(rot_ready, 1)
                if sines:
                    dve.wait_ge(rot_ready, 2 * (i - B + 1))
                    dve.tensor_tensor(qk_full[:], rot_a[:], rot_b[:], ALU.add).then_inc(full_ready, 1)

            def add_bv(i):
                b = i % B
                dve.wait_ge(pv_done, pv_number(i - B, 3, 1) + 1)
                if i == B:
                    dve.wait_ge(wide_loaded, 16)
                filled(dve, "v", i)
                ins = dve.tensor_tensor(v_sb[:, b * NT:(b + 1) * NT, :, 0:HD],
                                        bank_of("v", i)[:, 0:T].rearrange("k (j h d) -> k j h d", j=NT, h=H),
                                        bv_row.rearrange("k (h d) -> k h d", h=H).unsqueeze(1)
                                        .to_broadcast([P, NT, H, HD]), ALU.add)
                ins.then_inc(v_ready, 1)

            def maxima(i, n, unit):
                qb, p, s0, heads, keys = unit
                number = s_number(i, n)
                if n == 0 and i >= 2:
                    dve.wait_ge(max_split, i - 1)
                dve.wait_ge(s_filled, number + 1)
                dve.tensor_reduce(row_max[:, i % 2, qb, p, s0:s0 + heads],
                                  s_bank[number % 2][:].rearrange("q (s k) -> q s k", s=heads), AX_X, ALU.max)\
                   .then_inc(max_done, 1)

            def normalise(i, qb):
                step = f"out_turn{qb}"
                filled(dve, step, i)
                if i >= 2 and qb == 0:
                    filled(dve, "on_turn", i - 2)
                o = bank_of(step, i)[:].rearrange("q (h w) -> q h w", h=H)
                link(dve.reciprocal(denom[:, qb, :], o[:, :, HD]))
                ins = dve.tensor_tensor(o_n[:, i % 2, qb, :].rearrange("q (h d) -> q h d", h=H), o[:, :, 0:HD],
                                        denom[:, qb, :].unsqueeze(2).to_broadcast([P, H, HD]), ALU.mult)
                ins.then_inc(on_ready, 1)

            def add_attention(i):
                layer, b = divmod(i, B)
                filled(dve, "proj", i)
                dve.wait_ge(x_bias_ready[0], i + 1)
                dve.tensor_tensor(xs[2 * layer + 1][:, b * NT:(b + 1) * NT, :],
                                  bank_of("proj", i)[:, 0:T].rearrange("t (j d) -> t j d", j=NT),
                                  x_bias[0][:, i % 2, :, :], ALU.add).then_inc(mid_ready, 1)

            def times_up(half, i):
                step = f"up{half}"
                if half == 0:
                    filled(dve, "down", i - 2)
                filled(dve, step, i)
                dve.wait_ge(gelu_ready, 2 * (i - B) + half + 1)
                dve.tensor_tensor(hidden[:, i % 2, 2 * half:2 * half + 2, :],
                                  bank_of(step, i)[:].rearrange("f (k t) -> f k t", k=2), gelu[:, half, :, :],
                                  ALU.mult).then_inc(hidden_ready, 1)

            def add_mlp_out(i):
                layer, b = divmod(i, B)
                filled(dve, "down", i)
                if layer == 0:
                    dve.wait_ge(x_bias_ready[1], i + 1)
                old = xs[3][:, b * NT:(b + 1) * NT, :] if layer else x_bias[1][:, i % 2, :, :]
                dve.tensor_tensor(xs[2 * layer + 2][:, b * NT:(b + 1) * NT, :],
                                  bank_of("down", i)[:, 0:T].rearrange("t (j d) -> t j d", j=NT),
                                  old, ALU.add).then_inc(end_ready, 1)

            for _, step, i, n in PROGRAMS["vector"]:
                if step == "maxima":
                    maxima(i, n, score_units(i)[n])
                elif step == "rows":
                    cond_silu()
                elif step == "mods":
                    norm_mods()
                elif step in ("gates0", "gates1"):
                    gate_rows(int(step[-1]))
                elif step == "times":
                    times()
                elif step == "times2":
                    times2()
                elif step in ("stats1", "stats2"):
                    stats(int(step[-1]) - 1, i)
                elif step in ("centre1", "centre2"):
                    centre(int(step[-1]) - 1, i)
                elif step in ("rotate0", "rotate1"):
                    rotate(i, step == "rotate1")
                elif step == "split":
                    split(i)
                elif step == "add_bv":
                    add_bv(i)
                elif step in ("normalise0", "normalise1"):
                    normalise(i, int(step[-1]))
                elif step == "add_attention":
                    add_attention(i)
                elif step in ("times_up0", "times_up1"):
                    times_up(int(step[-1]), i)
                elif step == "add_mlp":
                    add_mlp_out(i)

        @block.gpsimd
        def _(pool):
            links = [0]

            def link(ins):
                links[0] += 1
                ins.then_inc(pchain, 1)
                pool.wait_ge(pchain, links[0])

            def setup0():
                link(pool.memset(minus_half[:], -0.5))
                pool.memset(stacks[:, 0, 1, :, :].bitcast(F32), minus_one_pair).then_inc(minus_ones, 1)
                pool.wait_ge(loaded["early"], 16)
                pool.tensor_copy(ident_bf[:], ident).then_inc(casts_ready, 1)

            def cast_mask():
                pool.wait_ge(loaded["layer0"], 16)
                pool.tensor_copy(mask_bf[:], mask).then_inc(casts_ready, 1)

            def setup_b(b):
                if b:
                    pool.memset(stacks[:, b, 1, :, :].bitcast(F32), minus_one_pair).then_inc(minus_ones, 1)
                link(pool.memset(v_sb[:, b * NT:(b + 1) * NT, :, :], 0.0))
                pool.memset(v_sb[:, b * NT:(b + 1) * NT, :, HD:HD + 1], 1.0).then_inc(v_ones, 1)

            def setup_gated():
                pool.wait_ge(gates_ready, 2)
                pool.wait_ge(wide_loaded, 16)
                pool.tensor_tensor(w_projg[:], gates[:, 0, :, :], w_proj.unsqueeze(1).to_broadcast([P, B, D]), ALU.mult)
                link(pool.tensor_tensor(add_attn[:], gates[:, 0, :, :], bproj_row.unsqueeze(1).to_broadcast([P, B, D]),
                                        ALU.mult))
                ins = pool.tensor_tensor(add_mlp[:], gates[:, 1, :, :], b2_row.unsqueeze(1).to_broadcast([P, B, D]),
                                         ALU.mult)
                ins.then_inc(gated_ready, 1)
                for b in range(B):
                    ins = pool.tensor_tensor(w_2g[:, b, :, :], w_2, gates[:, 1, b, :].unsqueeze(1)
                                             .to_broadcast([P, FC, D]), ALU.mult)
                ins.then_inc(gated_ready, 1)

            def root(w, i):
                if i >= 2:
                    pool.wait_ge(xn_ready[w], NT * (i - 1))
                pool.wait_ge(stats_ready[w], i + 1)
                pool.tensor_tensor(rstd[:, w, i % 2, :], var_eps[:, w, i % 2, :], minus_half[:], ALU.pow)\
                    .then_inc(rstd_ready[w], 1)

            def add_bias(w, i):
                layer, b = divmod(i, B)
                if layer and w:
                    return
                if i >= 2:
                    pool.wait_ge(end_ready if w else mid_ready, i - 1)
                if i == 0 and w == 0:
                    pool.wait_ge(gated_ready, 1)
                bias = bo_row if layer else (add_mlp if w else add_attn)[:, b, :]
                pool.tensor_tensor(x_bias[w][:, i % 2, :, :], xs[2 * layer + w][:, b * NT:(b + 1) * NT, :],
                                   bias.unsqueeze(1).to_broadcast([P, NT, D]), ALU.add).then_inc(x_bias_ready[w], 1)

            def split_max(i):
                buf = i % 2
                pool.wait_ge(max_done, s_number(i + 1))
                if i >= 2:
                    filled(pool, "max_turn", i - 2)
                part = max_parts[:, buf].rearrange("q b p n s -> q (b p) n s")
                full, rest1 = (x.rearrange("q b p s -> q (b p) s") for x in (row_max[:, buf], max_rest[:, buf]))
                link(pool.tensor_copy(part[:, :, 0, :], full))
                link(pool.tensor_tensor(rest1, full, part[:, :, 0, :], ALU.subtract))
                link(pool.tensor_copy(part[:, :, 1, :], rest1))
                pool.tensor_tensor(part[:, :, 2, :], rest1, part[:, :, 1, :], ALU.subtract).then_inc(max_split, 1)

            def mask_probs(i, n, unit):
                gs, kb, parity = unit
                number = t_number(i, n)
                pool.wait_ge(exp_done, number + 1)
                v = probs[:, kb, 4 * gs[0] + parity:4 * gs[-1] + 4:2, kb * P:(kb + 1) * P]
                pool.affine_select(out=v, in_=v, pattern=[[0, 2 * len(gs)], [1, P]], compare_op=ALU.is_ge, fill=0.0,
                    base=0, channel_multiplier=-1).then_inc(masked, 1)

            minus_one_pair = float(np.frombuffer(np.uint32(0xBF80BF80).tobytes(), np.float32)[0])
            for _, step, i, n in PROGRAMS["gpsimd"]:
                if step == "mask_probs":
                    mask_probs(i, n, prob_units(i)[n])
                elif step == "start":
                    setup0()
                elif step == "cast_mask":
                    cast_mask()
                elif step == "gated":
                    setup_gated()
                elif step in ("root1", "root2"):
                    root(int(step[-1]) - 1, i)
                elif step == "set_ones":
                    setup_b(i)
                elif step == "split_max":
                    split_max(i)
                elif step in ("add_bias1", "add_bias2"):
                    add_bias(int(step[-1]) - 1, i)


def turned(n):
    return n.reshape(*n.shape[:-1], HALF, 2, HD).swapaxes(-3, -2).swapaxes(-2, -1).reshape(n.shape)


def rotated(n):
    return n.reshape(*n.shape[:-1], H, 2, HD // 2)[..., ::-1, :].reshape(n.shape)


def laid_out(v):
    inv = (1.0 / 10000.0 ** (np.arange(0, HD, 2, dtype=np.float32) / np.float32(HD))).astype(np.float32)
    angle = (np.arange(T, dtype=np.float32)[:, None] * inv[None, :]).astype(np.float32)
    d = (np.arange(P) // HALF) % HD
    sign = np.where(d < HD // 2, np.float32(-1), np.float32(1))
    cos, sin = (f(angle).astype(np.float32)[:, d % (HD // 2)].T for f in (np.cos, np.sin))
    ahead = np.arange(P)[None, :] > np.arange(P)[:, None]
    chunks = lambda w: w.reshape(FC, P, D).transpose(1, 0, 2).reshape(P, FC * D)
    qkv = v["L0_cond_Wqkv"]
    bq, bk = v["L1_cond_bq"], v["L1_cond_bk"]
    vectors = {"turned bq": turned(bq), "turned bk": turned(bk),
               "rotated bq": turned(rotated(bq)), "rotated bk": turned(rotated(bk))}
    bada = v["L0_cond_bada"]
    rows = [vectors[name] if name in vectors else v[name] for name, _ in ROWS]
    return {
        "x": v["x"],
        "rows": np.concatenate([r.reshape(-1, D) for r in rows]),
        "wide": np.concatenate([bada[2 * D:3 * D], bada[5 * D:], *(v[name] for name in WIDE[2:])]),
        "early": np.concatenate([np.eye(P, dtype=np.float32), turned(qkv[:, :D]), turned(qkv[:, D:2 * D]),
                                 qkv[:, 2 * D:], v["L0_cond_Wada"]], axis=1),
        "layer0": np.concatenate([np.where(ahead, np.float32(MASKED), np.float32(0)), v["L0_cond_Wproj"],
                                  v["L0_cond_W1"], chunks(v["L0_cond_W2"])], axis=1),
        "attn1": np.concatenate([cos, sin * sign[:, None], turned(v["L1_cond_wq"]), turned(v["L1_cond_wk"]),
                                 turned(rotated(v["L1_cond_wq"])), turned(rotated(v["L1_cond_wk"])),
                                 v["L1_cond_t1_w1"], v["L1_cond_t2_w1"], v["L1_cond_t1_w2"], v["L1_cond_t2_w2"],
                                 v["L1_cond_wv"], v["L1_cond_wo"]], axis=1),
        "mlp1": np.concatenate([v["L1_cond_w_gate"], v["L1_cond_w_up"], chunks(v["L1_cond_w_down"])], axis=1),
    }


def kernel(**inputs):
    import concourse.bacc as _bacc
    from concourse.bass_utils import run_bass_kernel_spmd as _run

    nc = _bacc.Bacc("TRN2", target_bir_lowering=False, num_devices=1)
    arrays, a = {}, {}
    for name, value in laid_out({k: np.asarray(v) for k, v in inputs.items()}).items():
        v = np.ascontiguousarray(value)
        arrays[f"in_{name}"] = v
        a[name] = nc.dram_tensor(f"in_{name}", v.shape, mybir.dt.from_np(v.dtype), kind="ExternalInput").ap()
    out = nc.dram_tensor("out_0", (B, T, D), F32, kind="ExternalOutput").ap()
    build(nc, a, out)
    r = _run(nc, [arrays], core_ids=[0])
    return r.results[0]["out_0"]
```

```python
from contextlib import ExitStack

import numpy as np

import concourse.bass as bass
from concourse import mybir

ALU = mybir.AluOpType
ACT = mybir.ActivationFunctionType
F32 = mybir.dt.float32
BF16 = mybir.dt.bfloat16
AX_X = mybir.AxisListType.X

P = 128
B, T, D = 4, 256, 128
H, HD = 16, 8
NT = T // P
LAYERS = 2
ITEMS = LAYERS * B
FF = 512
FC = FF // P
EPS = 1e-5
SCALE = HD ** -0.5
MASKED = -1e30
HALF = H // 2
MS = HALF // 2
GROUPS = [(0, 0), (0, 1), (1, 0), (1, 1), (0, 2), (1, 2), (2, 0)]
NG = len(GROUPS)
SROWS = NG * HD
MROWS = SROWS + 3
STACK_DMAS = 2 * NG
MAX_DMAS = 2
VW = 32

ROWS = [("cond_1024", 4), ("L0_cond_bada", 6), ("L0_cond_g1", 1), ("L0_cond_be1", 1),
        ("L0_cond_g2", 1), ("L0_cond_be2", 1), ("L0_cond_b1", 4), ("L1_cond_w_norm1", 1),
        ("L1_cond_w_norm2", 1), ("L1_cond_t1_b1", 1), ("L1_cond_t2_b1", 1),
        ("L1_cond_t1_b2", 2), ("L1_cond_t2_b2", 2), ("turned bq", 1), ("turned bk", 1),
        ("rotated bq", 1), ("rotated bk", 1)]
NROWS = sum(n for _, n in ROWS)
PACKS = {
    "ident": [("ident", P)],
    "early": [("w_qk", 2 * D), ("w_v", D)],
    "ada": [("w_ada", 6 * D)],
    "layer0": [("mask", P), ("w_proj", D), ("w_1", FF), ("w_2", FF)],
    "attn1": [("rope", 2 * T), ("w_qk", 2 * D), ("w_rot", 2 * D), ("t_w1", 2 * D), ("t_w2", 4 * D), ("w_v", D), ("w_o", D)],
    "mlp1": [("w_gate", FF), ("w_up", FF), ("w_down", FF)],
}
WIDE = ["gate of attention", "gate of MLP", "L0_cond_bproj", "L0_cond_b2", "L1_cond_bv", "L1_cond_bo"]
COL = {name: sum(n for _, n in ROWS[:k]) for k, (name, _) in enumerate(ROWS)}


def score_units(i):
    units = []
    for s0 in range(0, HALF, MS):
        for qb in range(NT):
            keys = (qb + 1) * P if i < B else T
            n = 512 // keys
            units += [(qb, p, s, n, keys) for s in range(s0, s0 + MS, n) for p in range(2)]
    return units


def prob_units(i):
    if i < B:
        return [u for g in (0, 2) for u in
                [((g + k,), 0, p) for k in range(2) for p in range(2)] + [((g, g + 1), 1, p) for p in range(2)]]
    return [((g,), kb, p) for g in range(4) for kb in range(NT) for p in range(2)]


PRE_AT = [5, 9, 17, 30, 61, 75.5, 89.5, 109.5]
S_AT = [13, 26, 38, 51.5, 69, 88, 103, 118]
T_AT = [31, 43, 58, 71, 88, 106, 121, 138]
STEPS = {
    "tensor": {"turn1": ("pre", 1.4), "start qk": ("pre", 2.19), "qk": ("pre", 2.2), "start qk_rot": ("pre", 2.29),
               "qk_rot": ("pre", 2.4), "v": ("pre", 2.5), "max_turn0": ("half", 1.4), "max_turn1": ("max", 2.4),
               "out_turn0": ("post", 0.3), "out_turn1": ("post", 1.5), "on_turn": ("post", 3.1), "proj": ("post", 5),
               "turn2": ("post", 6.5), "start gate0": ("post", 8.19), "gate0": ("post", 8.2),
               "start hidden0": ("post", 8.29), "hidden0": ("post", 8.3), "start up0": ("post", 8.39),
               "up0": ("post", 8.4), "start gate1": ("post", 8.49), "gate1": ("post", 8.5),
               "start up1": ("post", 8.59), "up1": ("post", 8.7), "start hidden1": ("post", 8.79),
               "hidden1": ("post", 8.9), "start down": ("post", 10.29), "down": ("post", 10.4)},
    "scalar": {"affine1": ("pre", 1), "high": ("pre", 2.9), "copy_v": ("pre", 6.2), "move_max0": ("half", 1.9),
               "move_max1": ("max", 1.7), "copy_on": ("post", 3.4), "affine2": ("post", 6.4), "gelu0": ("post", 8.5),
               "gelu1": ("post", 8.9)},
    "vector": {"stats1": ("pre", -1), "centre1": ("pre", 0.6), "rotate0": ("pre", 2.2), "rotate1": ("pre", 2.3),
               "split": ("pre", 2.5), "add_bv": ("pre", 2.5), "middle": ("pre", 2.501), "low": ("pre", 3.2),
               "normalise0": ("post", 1.6), "normalise1": ("post", 1.6), "add_attention": ("post", 4.4),
               "stats2": ("post", 4.6), "centre2": ("post", 5.9), "times_up0": ("post", 7.1),
               "times_up1": ("post", 7.7), "add_mlp": ("post", 12.4)},
    "gpsimd": {"root1": ("pre", -2.9), "set_ones": ("pre", 2.9), "split_max0": ("half", 0),
               "split_max1": ("max", 1.2), "add_bias1": ("max", 15), "root2": ("post", 5.2),
               "add_bias2": ("post", 11.3)},
    "sync": {"stack0": ("pre", 2.6), "stack1": ("pre", 5.31), "stack2": ("pre", 8.02), "place_max0": ("half", 1.82),
             "place_max1": ("max", 5.22), "store": ("post", 21.7)},
}
ONLY = {"qk_rot": 1, "rotate0": 1, "rotate1": 1, "add_bv": 1, "copy_v": 0, "hidden0": 0, "hidden1": 0,
        "gate0": 1, "up0": 1, "gate1": 1, "up1": 1, "times_up0": 1, "times_up1": 1, "set_ones": 0,
        "add_bias2": 0, "store": 1}
SETUP = {
    "tensor": {"rows": -0.6, "mods": 3.4, "gates0": 7.4, "gates1": 8.5, "times": 24.7, "times2": 25.3},
    "scalar": {"rows": -6.9, "times": 25.5, "gelu_table": 144},
    "vector": {"rows": -8.1, "mods": 1.2, "gates0": 8.9, "gates1": 9, "times": 24.5, "times2": 25.1},
    "gpsimd": {"start": -102, "cast_mask": 3.5, "gated": 13.4},
    "sync": {"loads": 1.6, "late_loads": 4.6},
}
PV_LAG = 2.2
SCORES, MAXIMA, SCORES_T = 0.2, 1.2, 0

S_PACE = [1.05, 1, 1.2, 1.05, 1, 1, 1, 1.1]
T_PACE = [1, 1, 1, 1, 1, 1, 1, 1]
SHIFTS = {
    "tensor": {
        ("down", 1, 0): 1.6, ("down", 5, 0): 3.5, ("down", 6, 0): 4, ("gate0", 5, 0): 0.196,
        ("hidden0", 0, 0): 0.1, ("hidden1", 2, 0): 1, ("max_turn0", 1, 0): -0.3, ("max_turn0", 7, 0): -1,
        ("max_turn1", 1, 0): 0.6, ("max_turn1", 2, 0): 0.2, ("max_turn1", 6, 0): 1, ("on_turn", 1, 0): -0.5,
        ("on_turn", 5, 0): -1, ("out_turn1", 2, 0): 1, ("proj", 0, 0): -1, ("proj", 1, 0): -2,
        ("proj", 4, 0): -0.1, ("proj", 5, 0): -1.1, ("pv", 0, (0, 0)): -1.203, ("pv", 0, (2, 0)): -1,
        ("pv", 0, (2, 1)): -0.1, ("pv", 0, (3, 0)): -0.9, ("pv", 0, (3, 1)): -0.1, ("pv", 2, (0, 0)): -1.691,
        ("pv", 2, (0, 1)): -1.701, ("pv", 2, (1, 0)): -2, ("pv", 2, (1, 1)): -0.7, ("pv", 2, (2, 0)): -2.001,
        ("pv", 2, (2, 1)): -1, ("pv", 2, (3, 1)): -0.003, ("pv", 3, (0, 0)): -0.21, ("pv", 3, (1, 0)): -0.691,
        ("pv", 3, (1, 1)): -0.701, ("pv", 4, (3, 0)): -1, ("pv", 4, (3, 1)): -1, ("pv", 5, (0, 0)): 1,
        ("pv", 5, (1, 0)): -0.2, ("pv", 5, (1, 1)): -0.1, ("pv", 5, (2, 1)): 1.789, ("pv", 5, (3, 0)): 1,
        ("pv", 5, (3, 1)): -0.1, ("pv", 6, (0, 0)): 0.8, ("pv", 6, (1, 0)): 1, ("pv", 6, (1, 1)): -0.701,
        ("pv", 6, (2, 0)): -0.79, ("pv", 6, (2, 1)): -0.913, ("pv", 7, (1, 0)): -1, ("pv", 7, (1, 1)): -0.8,
        ("pv", 7, (2, 0)): -1, ("pv", 7, (3, 0)): -1.2, ("pv", 7, (3, 1)): -3, ("scores", 0, 6): -0.5,
        ("scores", 1, 10): 0.1, ("scores", 1, 2): -1, ("scores", 1, 6): 0.2, ("scores", 2, 1): 1,
        ("scores", 2, 10): -0.2, ("scores", 2, 11): -1, ("scores", 2, 4): -1, ("scores", 2, 5): -0.01,
        ("scores", 2, 6): -1, ("scores", 2, 7): -1, ("scores", 2, 8): -1, ("scores", 2, 9): -2,
        ("scores", 3, 1): 0.56, ("scores", 3, 11): -0.2, ("scores", 3, 2): -0.4, ("scores", 3, 3): 0.1,
        ("scores", 3, 4): -0.6, ("scores", 3, 5): -1.6, ("scores", 3, 6): -2, ("scores", 3, 7): -1.8,
        ("scores", 3, 8): -0.1, ("scores", 4, 14): -1, ("scores", 4, 15): -2, ("scores", 4, 4): -0.992,
        ("scores", 4, 5): -1.9, ("scores", 4, 6): -1.1, ("scores", 4, 9): -0.201, ("scores", 5, 0): -1.691,
        ("scores", 5, 11): -1, ("scores", 5, 14): 1, ("scores", 5, 2): -1, ("scores", 5, 3): -0.3,
        ("scores", 5, 4): -1, ("scores", 5, 5): 0.2, ("scores", 5, 7): -1, ("scores", 6, 10): -0.1,
        ("scores", 6, 11): -0.5, ("scores", 6, 3): -1, ("scores", 6, 4): -0.7, ("scores", 7, 10): -1,
        ("scores", 7, 11): -0.791, ("scores", 7, 12): -1.891, ("scores", 7, 13): -1.3, ("scores", 7, 14): -0.3,
        ("scores", 7, 4): -1.1, ("scores", 7, 5): -2, ("scores", 7, 6): -1.6, ("scores", 7, 7): -2.69,
        ("scores_t", 0, 0): -6, ("scores_t", 0, 1): -5, ("scores_t", 0, 10): -1, ("scores_t", 0, 11): -0.8,
        ("scores_t", 0, 2): -1, ("scores_t", 0, 3): -1.5, ("scores_t", 0, 4): -2, ("scores_t", 0, 6): -0.799,
        ("scores_t", 0, 7): -1.1, ("scores_t", 0, 8): -2, ("scores_t", 0, 9): -1, ("scores_t", 1, 11): -0.7,
        ("scores_t", 1, 2): -0.8, ("scores_t", 1, 3): -1.8, ("scores_t", 1, 4): -1.8, ("scores_t", 1, 5): -2.5,
        ("scores_t", 1, 7): -1, ("scores_t", 1, 8): -0.79, ("scores_t", 1, 9): -0.5, ("scores_t", 2, 0): -3.149,
        ("scores_t", 2, 10): -2.201, ("scores_t", 2, 2): -1, ("scores_t", 2, 6): -1, ("scores_t", 2, 7): -1.5,
        ("scores_t", 2, 8): -0.8, ("scores_t", 2, 9): -1.3, ("scores_t", 3, 0): -1.9, ("scores_t", 3, 1): -2.8,
        ("scores_t", 3, 2): -0.8, ("scores_t", 3, 3): -1.7, ("scores_t", 3, 4): -1, ("scores_t", 3, 6): -0.8,
        ("scores_t", 3, 8): -0.5, ("scores_t", 4, 0): -2.7, ("scores_t", 4, 1): -3, ("scores_t", 4, 11): -1,
        ("scores_t", 4, 2): -1, ("scores_t", 4, 3): -0.2, ("scores_t", 4, 4): -1.1, ("scores_t", 4, 6): -0.5,
        ("scores_t", 5, 1): -0.493, ("scores_t", 5, 13): -1, ("scores_t", 5, 14): -1, ("scores_t", 5, 15): -0.1,
        ("scores_t", 5, 7): -0.6, ("scores_t", 6, 1): -0.4, ("scores_t", 6, 10): -1.5, ("scores_t", 6, 11): -1,
        ("scores_t", 6, 12): -1.59, ("scores_t", 6, 13): -1, ("scores_t", 6, 14): -1, ("scores_t", 6, 3): -0.7,
        ("scores_t", 6, 4): -1, ("scores_t", 6, 6): -1, ("scores_t", 6, 7): -1, ("scores_t", 6, 8): -1,
        ("scores_t", 6, 9): -1, ("scores_t", 7, 0): -1.1, ("scores_t", 7, 1): -2, ("scores_t", 7, 10): -2,
        ("scores_t", 7, 11): -0.701, ("scores_t", 7, 15): -1, ("scores_t", 7, 2): -1.7, ("scores_t", 7, 4): -1,
        ("scores_t", 7, 5): 0.1, ("scores_t", 7, 7): -0.491, ("scores_t", 7, 8): -1.491, ("scores_t", 7, 9): -1,
        ("start down", 0, 0): 0.1, ("start hidden0", 2, 0): -1, ("start qk", 2, 0): -1, ("start qk", 6, 0): -0.2,
        ("start qk", 7, 0): -0.2, ("times2", 0, 0): 1.9, ("turn1", 2, 0): -4, ("turn1", 3, 0): -2,
        ("turn1", 5, 0): -0.8, ("turn2", 0, 0): 1, ("v", 6, 0): 1},
    "scalar": {
        ("affine1", 3, 0): 1, ("affine2", 2, 0): 0.5, ("copy_o", 2, 0): -0.7, ("copy_o", 5, 1): -1,
        ("copy_o", 6, 0): -1, ("copy_o", 7, 0): -0.6, ("copy_on", 1, 0): -1, ("copy_on", 6, 0): -1,
        ("copy_v", 0, 0): -2, ("copy_v", 3, 0): 2, ("exp", 0, 1): -1, ("exp", 0, 2): -0.8, ("exp", 0, 9): -0.3,
        ("exp", 2, 0): -1, ("exp", 2, 6): -1, ("exp", 2, 8): -1, ("exp", 3, 2): -1, ("exp", 3, 8): -0.4,
        ("exp", 4, 0): -1, ("exp", 4, 1): -1, ("exp", 4, 4): -1, ("exp", 4, 5): -1, ("exp", 6, 1): -1,
        ("exp", 6, 10): -2, ("exp", 6, 11): -1, ("exp", 6, 5): 1, ("exp", 6, 9): -1, ("exp", 7, 0): -1,
        ("exp", 7, 7): -1, ("exp", 7, 8): -2, ("exp", 7, 9): -1, ("gelu1", 1, 0): -0.3,
        ("gelu_table", 0, 0): -12.6, ("high", 4, 0): -0.7, ("move_max0", 1, 0): 1, ("move_max0", 3, 0): -0.5,
        ("move_max0", 4, 0): -0.4, ("move_max0", 5, 0): 3, ("move_max1", 6, 0): 1},
    "vector": {
        ("add_bv", 5, 0): -0.1, ("add_bv", 6, 0): -0.1, ("add_bv", 7, 0): 0.1, ("add_mlp", 0, 0): 0.2,
        ("add_mlp", 4, 0): -1, ("add_mlp", 5, 0): 1, ("centre1", 0, 0): -6, ("centre1", 1, 0): -2,
        ("centre1", 2, 0): -8.7, ("centre1", 3, 0): -3, ("centre1", 4, 0): -3, ("centre1", 5, 0): -4,
        ("centre1", 6, 0): -3, ("centre1", 7, 0): -4, ("centre2", 1, 0): 0.5, ("low", 2, 0): 4,
        ("maxima", 0, 6): -1, ("maxima", 1, 6): -0.7, ("maxima", 1, 7): -1, ("maxima", 3, 11): -0.75,
        ("maxima", 3, 5): -1, ("maxima", 3, 6): -0.4, ("maxima", 4, 1): 1, ("maxima", 4, 4): -1,
        ("maxima", 4, 5): -1.591, ("maxima", 4, 7): -1, ("maxima", 5, 1): -1, ("maxima", 5, 3): -1,
        ("maxima", 5, 4): -1.2, ("maxima", 6, 10): -2.1, ("maxima", 6, 8): -1, ("maxima", 6, 9): -1.2,
        ("maxima", 7, 10): -1, ("maxima", 7, 11): -1.291, ("maxima", 7, 12): -2.3, ("maxima", 7, 13): -3.4,
        ("maxima", 7, 5): -1, ("maxima", 7, 9): -1, ("middle", 0, 0): 0.3, ("middle", 2, 0): 3,
        ("normalise0", 2, 0): -0.1, ("normalise0", 4, 0): -0.5, ("normalise1", 5, 0): 2, ("split", 0, 0): 0.3,
        ("split", 3, 0): -0.1, ("stats1", 0, 0): -7, ("stats1", 1, 0): -2, ("stats1", 2, 0): -9,
        ("stats1", 3, 0): -20.1, ("stats1", 4, 0): -2, ("stats1", 5, 0): -5, ("stats1", 6, 0): -2,
        ("stats1", 7, 0): -6, ("stats2", 1, 0): 1, ("times", 0, 0): -0.8, ("times2", 0, 0): 2},
    "gpsimd": {
        ("add_bias1", 0, 0): -26, ("add_bias1", 1, 0): -35, ("add_bias1", 2, 0): -14, ("add_bias1", 3, 0): -13,
        ("add_bias1", 4, 0): -24, ("add_bias1", 5, 0): -23, ("add_bias1", 6, 0): -20, ("add_bias1", 7, 0): -23,
        ("add_bias2", 0, 0): -4, ("add_bias2", 2, 0): -4, ("add_bias2", 3, 0): -5, ("mask_probs", 0, 0): -1,
        ("root1", 0, 0): -6, ("root1", 2, 0): -4, ("root1", 4, 0): -1, ("root1", 5, 0): -3, ("root1", 6, 0): -1,
        ("root1", 7, 0): -5, ("root2", 1, 0): 1, ("set_ones", 0, 0): -10, ("set_ones", 1, 0): -3,
        ("set_ones", 2, 0): -7, ("set_ones", 3, 0): -19, ("split_max0", 3, 0): 1, ("split_max0", 5, 0): 1,
        ("split_max1", 0, 0): 2, ("split_max1", 2, 0): -0.5},
    "sync": {
        ("place_max0", 4, 0): -0.5, ("place_max0", 6, 0): 9, ("place_max0", 7, 0): -2, ("stack1", 7, 0): -1,
        ("stack2", 0, 0): -2, ("stack2", 5, 0): -5},
}


def programs():
    out = {engine: [(t, step, 0, 0) for step, t in steps.items()] for engine, steps in SETUP.items()}
    for i in range(ITEMS):
        s_units, t_units = score_units(i), prob_units(i)
        for n in range(len(s_units)):
            out["tensor"].append((S_AT[i] + n * S_PACE[i] + SCORES, "scores", i, n))
            out["vector"].append((S_AT[i] + n * S_PACE[i] + MAXIMA, "maxima", i, n))
        pv_at = {}
        for n, (groups, kb, _) in enumerate(t_units):
            t = T_AT[i] + n * T_PACE[i]
            out["tensor"].append((t + SCORES_T, "scores_t", i, n))
            out["scalar"].append((t, "exp", i, n))
            if i < B:
                out["gpsimd"].append((t, "mask_probs", i, n))
            for g in groups:
                for k in (0, 1) if i < B and kb else (kb,):
                    pv_at[g, k] = t + PV_LAG + (g % 2 if i < B else 0) + 0.01 * k
        for (g, kb), t in pv_at.items():
            out["tensor"].append((t, "pv", i, (g, kb)))
            if g % 2 and kb:
                out["scalar"].append((t + 0.05, "copy_o", i, g // 2))
        base = {"pre": PRE_AT[i], "half": S_AT[i] + len(s_units) // 2 * S_PACE[i],
                "max": S_AT[i] + len(s_units) * S_PACE[i], "post": max(pv_at.values()) - 0.2}
        for engine, steps in STEPS.items():
            out[engine] += [(base[b] + t, step, i, 0)
                            for step, (b, t) in steps.items() if ONLY.get(step.split()[-1], i // B) == i // B]
    return {engine: sorted(((t + SHIFTS.get(engine, {}).get((step, i, n), 0), step, i, n) for t, step, i, n in steps),
                           key=lambda x: x[0]) for engine, steps in out.items()}


PROGRAMS = programs()

S_BANKS, T_BANKS, M_BANKS = 3, 2, 2
USE = {(step, i): n for n, (step, i) in enumerate(
    (step, i) for _, step, i, _ in PROGRAMS["tensor"]
    if step not in ("scores", "scores_t", "pv") and not step.startswith("start"))}
BANK_STEPS = list(USE)


def s_number(i, n=0):
    return sum(len(score_units(j)) for j in range(i)) + n


def t_number(i, n=0):
    return sum(len(prob_units(j)) for j in range(i)) + n


def t_done(i, g, kb):
    return t_number(i) + max(n + 1 for n, u in enumerate(prob_units(i)) if g in u[0] and u[1] == kb)


def pv_number(i, g, kb):
    return (i * 4 + g) * NT + kb


def build(nc, a, out):
    with ExitStack() as ctx:
        def sb(name, shape, dt=F32):
            return ctx.enter_context(nc.sbuf_tensor(name, shape, dt))

        def sem(name):
            return ctx.enter_context(nc.semaphore(name))

        banks = [ctx.enter_context(nc.psum_tensor(f"bank{k}", [P, 512], F32)) for k in range(8)]
        s_bank, t_bank, o_bank, m_bank = banks[:S_BANKS], banks[S_BANKS:-M_BANKS - 1], banks[-M_BANKS - 1], banks[-M_BANKS:]

        packs = {name: sb(f"pack_{name}", [P, sum(n for _, n in held)]) for name, held in PACKS.items()}

        def packed(pack, name):
            at = 0
            for held, n in PACKS[pack]:
                if held == name:
                    return packs[pack][:, at:at + n]
                at += n

        ident = packed("ident", "ident")
        w_ada = packed("ada", "w_ada").rearrange("p (k d) -> p k d", k=6)
        w_qk = [packed(name, "w_qk").rearrange("p (k d) -> p k d", k=2) for name in ("early", "attn1")]
        w_v = [packed(name, "w_v") for name in ("early", "attn1")]
        mask = packed("layer0", "mask")
        w_proj = packed("layer0", "w_proj")
        w_1 = packed("layer0", "w_1")
        w_2 = packed("layer0", "w_2").rearrange("p (c d) -> p c d", c=FC)
        rope = packed("attn1", "rope").rearrange("p (k t) -> p k t", k=2)
        w_rot = packed("attn1", "w_rot").rearrange("p (k d) -> p k d", k=2)
        t_w1 = packed("attn1", "t_w1").rearrange("p (k d) -> p k d", k=2)
        t_w2 = packed("attn1", "t_w2").rearrange("p (k n d) -> p k n d", k=2, n=2)
        w_o = packed("attn1", "w_o")
        w_gate = packed("mlp1", "w_gate")
        w_up = packed("mlp1", "w_up")
        w_down = packed("mlp1", "w_down").rearrange("p (c d) -> p c d", c=FC)
        rows = sb("rows", [NROWS, P])
        cols = sb("cols", [P, NROWS])
        wide = sb("wide", [P, len(WIDE), D])
        bproj_row, b2_row, bv_row, bo_row = (wide[:, k, :] for k in range(2, 6))
        ident_bf = sb("ident_bf", [P, P], BF16)
        mask_bf = sb("mask_bf", [P, P], BF16)
        silu = sb("silu", [P, 4, B])
        silu_wide = sb("silu_wide", [P, B, P])
        mod = sb("mod", [P, 4, B])
        gates = sb("gates", [P, 2, B, D])
        tsilu = sb("tsilu", [P, 5, 2, B])
        tmod = sb("tmod", [P, 2, 2, B])
        mul_c = sb("mul_c", [P, LAYERS, 2, B])
        add_c = sb("add_c", [P, LAYERS, 2, B])
        w_projg = sb("w_projg", [P, B, D])
        w_2g = sb("w_2g", [P, B, FC, D])
        add_attn = sb("add_attn", [P, B, D])
        add_mlp = sb("add_mlp", [P, B, D])
        xs = [sb(f"x{k}", [P, B * NT, D]) for k in range(2 * LAYERS)]
        xs.append(xs[0])
        bn = sb("bn", [P, 2, NT, 6])
        mean_var = sb("mean_var", [P, 2, 2, NT, 2])
        var_eps = sb("var_eps", [P, 2, 2, NT])
        rstd = sb("rstd", [P, 2, 2, NT])
        minus_half = sb("minus_half", [P, NT])
        square = sb("square", [P, NT])
        unused = sb("unused", [P, NT])
        xn = [sb(f"xn{w}", [P, 2, NT, D]) for w in range(2)]
        x_bias = [sb(f"x_bias{w}", [P, 2, NT, D]) for w in range(2)]
        xmt = [sb(f"xmt{w}", [P, 2, T]) for w in range(2)]
        rot_a = sb("rot_a", [P, 2, T])
        rot_b = sb("rot_b", [P, 2, T])
        qk_full = sb("qk_full", [P, 2, T])
        rest = sb("rest", [P, 2, T])
        parts = sb("parts", [P, 2, 2 * 3, T], BF16)
        stacks = sb("stacks", [P, B, HALF, 2, T], BF16)
        v_sb = sb("v_sb", [P, B * NT, H, VW])
        row_max = sb("row_max", [P, 2, 2, NT, 2, MS])
        max_rest = sb("max_rest", [P, 2, 2, NT, 2, MS])
        max_parts = sb("max_parts", [P, 2, 2, NT, 2, 3, MS], BF16)
        max_rows = sb("max_rows", [2 * 3 * MS, 2, 2, T], BF16)
        probs = sb("probs", [P, NT, H, T])
        o_t = sb("o_t", [P, 2, 4, T])
        denom = sb("denom", [P, NT, H])
        o_n = sb("o_n", [P, 2, NT, D])
        o_nt = sb("o_nt", [P, 2, T])
        gelu = sb("gelu", [P, 2, 2, T])
        hidden = sb("hidden", [P, 2, FC, T])

        x_loaded = [sem(f"x_loaded{b}") for b in range(B)]
        rows_loaded = sem("rows_loaded")
        loaded = {name: sem(f"{name}_loaded") for name in PACKS}
        wide_loaded = sem("wide_loaded")
        casts_ready = sem("casts_ready")
        minus_half_ready = sem("minus_half_ready")
        minus_ones = sem("minus_ones")
        v_ones = sem("v_ones")
        cols_ready = sem("cols_ready")
        neg_exp = sem("neg_exp")
        silu_ready = sem("silu_ready")
        norm0_ready = sem("norm0_ready")
        norm1_ready = sem("norm1_ready")
        wide_ready = sem("wide_ready")
        gates_ready = sem("gates_ready")
        gated_ready = sem("gated_ready")
        tz_ready = sem("tz_ready")
        texp_ready = sem("texp_ready")
        tsilu_ready = sem("tsilu_ready")
        vchain = sem("vchain")
        pchain = sem("pchain")
        stats_ready = [sem(f"stats_ready{w}") for w in range(2)]
        rstd_ready = [sem(f"rstd_ready{w}") for w in range(2)]
        xn_ready = [sem(f"xn_ready{w}") for w in range(2)]
        x_bias_ready = [sem(f"x_bias_ready{w}") for w in range(2)]
        xmt_ready = [sem(f"xmt_ready{w}") for w in range(2)]
        bank_filled = sem("bank_filled")
        high_ready = sem("high_ready")
        rest_ready = sem("rest_ready")
        middle_ready = sem("middle_ready")
        low_ready = sem("low_ready")
        full_ready = sem("full_ready")
        rot_ready = sem("rot_ready")
        stacks_loaded = [sem(f"stacks_loaded{i}") for i in range(ITEMS)]
        v_ready = sem("v_ready")
        s_filled = sem("s_filled")
        max_done = sem("max_done")
        max_split = sem("max_split")
        max_rows_ready = sem("max_rows_ready")
        max_rows_placed = [[sem(f"max_rows_placed{i}_{h}") for h in range(2)] for i in range(ITEMS)]
        t_filled = sem("t_filled")
        exp_done = sem("exp_done")
        masked = sem("masked")
        pv_done = sem("pv_done")
        o_copied = sem("o_copied")
        on_ready = sem("on_ready")
        ont_ready = sem("ont_ready")
        mid_ready = sem("mid_ready")
        gelu_ready = sem("gelu_ready")
        hidden_ready = sem("hidden_ready")
        end_ready = sem("end_ready")
        out_stored = sem("out_stored")

        block = ctx.enter_context(nc.Block())

        def bank_of(step, i):
            return m_bank[USE[step, i] % M_BANKS]

        def filled(eng, step, i):
            eng.wait_ge(bank_filled, USE[step, i] + 1)

        def col(name, k=0):
            return cols[:, COL[name] + k:COL[name] + k + 1]

        @block.sync
        def _(sp):
            def load(dst, name, signal):
                sp.dma_start(dst, a[name] if isinstance(name, str) else name).then_inc(signal, 16)

            def load_x(b):
                load(xs[0][:, b * NT:(b + 1) * NT, :], a["x"][b].rearrange("(j p) d -> p j d", p=P), x_loaded[b])

            def first_loads():
                load(rows[:], "rows", rows_loaded)
                load(packs["ident"][:], "ident", loaded["ident"])
                load_x(0)
                load(packs["ada"][:], "ada", loaded["ada"])
                load(packs["early"][:], "early", loaded["early"])
                load_x(1)
                load(wide[:].rearrange("p k d -> p (k d)"), a["wide"].partition_broadcast(P), wide_loaded)
                load(packs["layer0"][:], "layer0", loaded["layer0"])
                for b in range(2, B):
                    load_x(b)

            def stack(part, i):
                b = i % B
                sp.wait_ge((high_ready, middle_ready, low_ready)[part], i + 1)
                if part == 0 and i < B:
                    sp.wait_ge(minus_ones, i + 1)
                if part == 0 and i >= B:
                    sp.wait_ge(s_filled, s_number(i - B + 1))
                    sp.wait_ge(t_filled, t_number(i - B + 1))
                for g, (pq, pk) in enumerate(GROUPS):
                    if max(pq, pk) == part:
                        for p in range(2):
                            row = 64 * p + g * HD
                            sp.dma_start(stacks[row:row + HD, b, :, :, :],
                                         parts[64 * p:64 * p + 64, i % 2, pq:pk + 4:pk + 3 - pq, :])\
                                .then_inc(stacks_loaded[i], 16)

            def place_max(i, half):
                b = i % B
                sp.wait_ge(max_rows_ready, 2 * i + half + 1)
                for p in range(2):
                    r, row = 3 * MS * p, 64 * p + SROWS
                    sp.dma_start(stacks[row:row + 3, b, half * MS:(half + 1) * MS, 0, :],
                                 max_rows[r:r + 3 * MS, i % 2, half, :]).then_inc(max_rows_placed[i][half], 16)

            for _, step, i, _ in PROGRAMS["sync"]:
                if step == "loads":
                    first_loads()
                elif step in ("stack0", "stack1", "stack2"):
                    stack(int(step[-1]), i)
                elif step == "late_loads":
                    for name in ("attn1", "mlp1"):
                        load(packs[name][:], name, loaded[name])
                elif step in ("place_max0", "place_max1"):
                    place_max(i, int(step[-1]))
                elif step == "store":
                    b = i % B
                    sp.wait_ge(end_ready, i + 1)
                    sp.dma_start(out[b].rearrange("(j p) d -> p j d", p=P),
                                 xs[4][:, b * NT:(b + 1) * NT, :]).then_inc(out_stored, 16)
            sp.wait_ge(out_stored, 16 * B)

        @block.tensor
        def _(pe):
            def reader_of(step, i):
                k = int(step[-1]) if step[-1].isdigit() else 0
                if step in ("turn1", "turn2"):
                    return xmt_ready[k - 1], i + 1
                return {
                    "rows": (cols_ready, 1), "mods": (norm0_ready, 1), "gates": (gates_ready, k + 1),
                    "times": (norm1_ready if k else tz_ready, 1),
                    "qk": (rot_ready, 2 * (i - B) + 1) if i >= B else (rest_ready, i + 1),
                    "qk_rot": (rot_ready, 2 * (i - B) + 2), "v": (v_ready, i + 1),
                    "max_turn": (max_rows_ready, 2 * i + k + 1), "out_turn": (on_ready, NT * i + k + 1),
                    "on_turn": (ont_ready, i + 1), "proj": (mid_ready, i + 1),
                    "hidden": (hidden_ready, 2 * i + k + 1), "gate": (gelu_ready, 2 * (i - B) + k + 1),
                    "up": (hidden_ready, 2 * i + k + 1), "down": (end_ready, i + 1),
                }[step.rstrip("012")]

            def take_bank(step, i):
                n = USE[step, i]
                if n >= M_BANKS:
                    pe.wait_ge(*reader_of(*BANK_STEPS[n - M_BANKS]))
                return m_bank[n % M_BANKS]

            def mm(o, lhs, rhs, start=True, stop=True):
                return pe.matmul(o, lhs, rhs, start=start, stop=stop)

            def rows_to_cols():
                bank = take_bank("rows", 0)
                pe.wait_ge(rows_loaded, 16)
                pe.wait_ge(loaded["ident"], 16)
                pe.transpose(bank[:, 0:NROWS], rows[:], ident[0:NROWS, 0:NROWS]).then_inc(bank_filled, 1)

            def mods():
                bank = take_bank("mods", 0)
                pe.wait_ge(silu_ready, 1)
                pe.wait_ge(loaded["ada"], 16)
                for n, chunk in enumerate((0, 1, 3, 4)):
                    last = mm(bank[:, n * B:(n + 1) * B], w_ada[:, chunk, :], silu[:, 3, :])
                last.then_inc(bank_filled, 1)

            def gate_rows(k):
                bank = take_bank(f"gates{k}", 0)
                pe.wait_ge(wide_ready, 1)
                for b in range(B):
                    last = mm(bank[:, b * D:(b + 1) * D], silu_wide[:, b, :], w_ada[:, 2 + 3 * k, :])
                last.then_inc(bank_filled, 1)

            def times():
                bank = take_bank("times", 0)
                pe.wait_ge(loaded["attn1"], 16)
                for k in range(2):
                    last = mm(bank[:, k * B:(k + 1) * B], t_w1[:, k, :], cols[:, 0:B])
                last.then_inc(bank_filled, 1)

            def times2():
                bank = take_bank("times2", 0)
                pe.wait_ge(tsilu_ready, 1)
                for k in range(2):
                    for n in range(2):
                        last = mm(bank[:, (2 * k + n) * B:(2 * k + n + 1) * B], t_w2[:, k, n, :], tsilu[:, 4, k, :])
                last.then_inc(bank_filled, 1)

            def turn(w, i):
                bank = take_bank(f"turn{w + 1}", i)
                for j in range(NT):
                    pe.wait_ge(xn_ready[w], NT * i + j + 1)
                    last = pe.transpose(bank[:, j * P:(j + 1) * P], xn[w][:, i % 2, j, :], ident)
                last.then_inc(bank_filled, 1)

            def project_qk(step, i, k):
                bank = bank_of(step, i) if k else take_bank(step, i)
                if i == 0 and k == 0:
                    pe.wait_ge(loaded["early"], 16)
                pe.wait_ge(xmt_ready[0], i + 1)
                w = w_rot if step == "qk_rot" else w_qk[i // B]
                last = mm(bank[:, k * T:(k + 1) * T], w[:, k, :], xmt[0][:, i % 2, :])
                if k:
                    last.then_inc(bank_filled, 1)

            def project_v(i):
                bank = take_bank("v", i)
                for j in range(NT):
                    last = mm(bank[:, j * D:(j + 1) * D], xmt[0][:, i % 2, j * P:(j + 1) * P], w_v[i // B])
                last.then_inc(bank_filled, 1)

            def scores(i, n, unit):
                qb, p, s0, heads, keys = unit
                b, number = i % B, s_number(i, n)
                bank = s_bank[number % S_BANKS]
                if n == 0:
                    pe.wait_ge(stacks_loaded[i], 16 * STACK_DMAS)
                if number == 0:
                    pe.wait_ge(casts_ready, 2)
                if number >= S_BANKS:
                    pe.wait_ge(max_done, number - S_BANKS + 1)
                r = slice(64 * p, 64 * p + SROWS)
                whole = i < B and keys == P
                if whole:
                    mm(bank[:].rearrange("q (h k) -> q h k", h=heads), ident_bf[:],
                       mask_bf[:].unsqueeze(1).to_broadcast([P, heads, P]), stop=False)
                for k in range(heads):
                    o = bank[:, k * keys:(k + 1) * keys]
                    last = mm(o, stacks[r, b, s0 + k, 0, qb * P:(qb + 1) * P], stacks[r, b, s0 + k, 1, 0:keys],
                              start=not whole, stop=i >= B or (whole and k == heads - 1))
                    if i < B and not whole:
                        last = mm(o[:, P:T], ident_bf[:], mask_bf[:], start=False)
                last.then_inc(s_filled, 1)

            def turn_max(i, half):
                bank = take_bank(f"max_turn{half}", i)[:].bitcast(BF16)
                pe.wait_ge(max_split, 2 * i + half + 1)
                for qb in range(NT):
                    last = pe.transpose(bank[0:2 * 3 * MS, qb * P:(qb + 1) * P],
                                        max_parts[:, i % 2, half, qb].rearrange("q p n s -> q (p n s)"), ident_bf[:])
                last.then_inc(bank_filled, 1)

            def scores_t(i, n, unit):
                gs, kb, parity = unit
                b, number = i % B, t_number(i, n)
                bank = t_bank[number % T_BANKS]
                if n in (0, len(prob_units(i)) // 2):
                    pe.wait_ge(max_rows_placed[i][min(n, 1)], 16 * MAX_DMAS)
                if number >= T_BANKS:
                    pe.wait_ge(exp_done, number - T_BANKS + 1)
                q0 = (len(gs) - 1) * P
                for k, (g, j) in enumerate((g, j) for g in gs for j in (parity, parity + 2)):
                    p, s = j % 2, 2 * g + j // 2
                    r = slice(64 * p, 64 * p + MROWS)
                    last = mm(bank[:, k * (T - q0):(k + 1) * (T - q0)],
                              stacks[r, b, s, 1, kb * P:(kb + 1) * P], stacks[r, b, s, 0, q0:T])
                last.then_inc(t_filled, 1)

            def pv(i, g, kb):
                b = i % B
                if g == 0 and kb == 0:
                    pe.wait_ge(v_ready, i + 1)
                if g % 2 == 0 and kb == 0 and 2 * i + g // 2 >= 1:
                    pe.wait_ge(o_copied, 2 * i + g // 2)
                if i < B:
                    pe.wait_ge(masked, t_done(i, g, kb))
                else:
                    pe.wait_ge(exp_done, t_done(i, g, kb))
                q0 = P if i < B and kb == 1 else 0
                bank = o_bank
                for j in range(4):
                    last = pe.matmul(bank[32 * j:32 * j + VW, (g % 2) * T + q0:(g % 2 + 1) * T],
                                     v_sb[:, b * NT + kb, 4 * g + j, :], probs[:, kb, 4 * g + j, q0:T],
                                     start=(kb == 0), stop=(kb == NT - 1), tile_position=(0, 32 * j))
                last.then_inc(pv_done, 1)

            def out_turn(i, qb):
                bank = take_bank(f"out_turn{qb}", i)
                pe.wait_ge(o_copied, 2 * (i + 1))
                for g in range(4):
                    last = pe.transpose(bank[:, g * P:(g + 1) * P], o_t[:, i % 2, g, qb * P:(qb + 1) * P], ident)
                last.then_inc(bank_filled, 1)

            def turn_out(i):
                bank = take_bank("on_turn", i)
                for j in range(NT):
                    pe.wait_ge(on_ready, NT * i + j + 1)
                    last = pe.transpose(bank[:, j * P:(j + 1) * P], o_n[:, i % 2, j, :], ident)
                last.then_inc(bank_filled, 1)

            def project_out(i):
                bank = take_bank("proj", i)
                if i == 0:
                    pe.wait_ge(gated_ready, 1)
                pe.wait_ge(ont_ready, i + 1)
                w = w_o if i >= B else w_projg[:, i % B, :]
                for j in range(NT):
                    last = mm(bank[:, j * D:(j + 1) * D], o_nt[:, i % 2, j * P:(j + 1) * P], w)
                last.then_inc(bank_filled, 1)

            def mlp_in(step, i, w, k):
                bank = bank_of(step, i) if k else take_bank(step, i)
                pe.wait_ge(xmt_ready[1], i + 1)
                if i == B:
                    pe.wait_ge(loaded["mlp1"], 16)
                c = 2 * int(step[-1]) + k
                last = mm(bank[:, k * T:(k + 1) * T], w[:, c * P:(c + 1) * P], xmt[1][:, i % 2, :])
                if k:
                    last.then_inc(bank_filled, 1)

            def mlp_out(i, j):
                bank = bank_of("down", i) if j else take_bank("down", i)
                if i == 0:
                    pe.wait_ge(gated_ready, 2)
                pe.wait_ge(hidden_ready, 2 * (i + 1))
                for c in range(FC):
                    w = w_down[:, c, :] if i >= B else w_2g[:, i % B, c, :]
                    last = mm(bank[:, j * D:(j + 1) * D], hidden[:, i % 2, c, j * P:(j + 1) * P], w,
                              start=(c == 0), stop=(c == FC - 1))
                if j:
                    last.then_inc(bank_filled, 1)

            for _, step, i, n in PROGRAMS["tensor"]:
                half = 0 if step.startswith("start") else 1
                step = step.split()[-1]
                if step == "scores_t":
                    scores_t(i, n, prob_units(i)[n])
                elif step == "pv":
                    pv(i, *n)
                elif step == "scores":
                    scores(i, n, score_units(i)[n])
                elif step == "rows":
                    rows_to_cols()
                elif step == "mods":
                    mods()
                elif step in ("gates0", "gates1"):
                    gate_rows(int(step[-1]))
                elif step == "times":
                    times()
                elif step == "times2":
                    times2()
                elif step in ("turn1", "turn2"):
                    turn(int(step[-1]) - 1, i)
                elif step in ("qk", "qk_rot"):
                    project_qk(step, i, half)
                elif step == "v":
                    project_v(i)
                elif step in ("max_turn0", "max_turn1"):
                    turn_max(i, int(step[-1]))
                elif step in ("out_turn0", "out_turn1"):
                    out_turn(i, int(step[-1]))
                elif step == "on_turn":
                    turn_out(i)
                elif step == "proj":
                    project_out(i)
                elif step in ("hidden0", "hidden1"):
                    mlp_in(step, i, w_1, half)
                elif step in ("gate0", "gate1"):
                    mlp_in(step, i, w_gate, half)
                elif step in ("up0", "up1"):
                    mlp_in(step, i, w_up, half)
                elif step == "down":
                    mlp_out(i, half)

        @block.scalar
        def _(act):
            def affine(w, i):
                layer, b = divmod(i, B)
                step = f"turn{w + 1}"
                if i == 0 and w == 0:
                    act.wait_ge(norm0_ready, 1)
                if i == B and w == 0:
                    act.wait_ge(norm1_ready, 1)
                if i >= 2:
                    filled(act, ("v" if w == 0 else "hidden1" if i - 2 < B else "up1"), i - 2)
                filled(act, step, i)
                ins = act.activation(xmt[w][:, i % 2, :], bank_of(step, i)[:, 0:T], ACT.Identity,
                                     bias=add_c[:, layer, w, b:b + 1], scale=mul_c[:, layer, w, b:b + 1])
                ins.then_inc(xmt_ready[w], 1)

            def high_part(i):
                if i >= 2:
                    act.wait_ge(stacks_loaded[i - 2], 16 * STACK_DMAS)
                filled(act, "qk", i)
                act.activation(parts[:, i % 2, 0:4:3, :], bank_of("qk", i)[:].rearrange("c (k t) -> c k t", k=2),
                               ACT.Copy).then_inc(high_ready, 1)

            def high_part1(i):
                act.wait_ge(full_ready, i - B + 1)
                act.wait_ge(stacks_loaded[i - 2], 16 * STACK_DMAS)
                act.activation(parts[:, i % 2, 0:4:3, :], qk_full[:], ACT.Copy).then_inc(high_ready, 1)

            def copy_v(i):
                b = i % B
                act.wait_ge(v_ones, i + 1)
                filled(act, "v", i)
                ins = act.activation(v_sb[:, b * NT:(b + 1) * NT, :, 0:HD],
                                     bank_of("v", i)[:, 0:T].rearrange("k (j h d) -> k j h d", j=NT, h=H), ACT.Copy)
                ins.then_inc(v_ready, 1)

            def move_max(i, half):
                if i >= 2:
                    act.wait_ge(max_rows_placed[i - 2][half], 16 * MAX_DMAS)
                filled(act, f"max_turn{half}", i)
                ins = act.activation(max_rows[:, i % 2, half, :],
                                     bank_of(f"max_turn{half}", i)[:].bitcast(BF16)[0:2 * 3 * MS, 0:T], ACT.Copy)
                ins.then_inc(max_rows_ready, 1)

            def exponentials(i, n, unit):
                gs, kb, parity = unit
                if i >= 1:
                    act.wait_ge(pv_done, pv_number(i, gs[-1], kb) - 4 * NT + 1)
                number = t_number(i, n)
                act.wait_ge(t_filled, number + 1)
                q0 = (len(gs) - 1) * P
                dst = probs[:, kb, 4 * gs[0] + parity:4 * gs[-1] + 4:2, q0:T]
                src = t_bank[number % T_BANKS][:].rearrange("k (h q) -> k h q", h=2 * len(gs))
                act.activation(dst, src, ACT.Exp, scale=SCALE).then_inc(exp_done, 1)

            def copy_o(i, pair):
                if i >= 2:
                    filled(act, "out_turn1", i - 2)
                act.wait_ge(pv_done, pv_number(i, 2 * pair + 1, 1) + 1)
                act.activation(o_t[:, i % 2, 2 * pair:2 * pair + 2, :],
                               o_bank[:].rearrange("r (g q) -> r g q", g=2), ACT.Copy).then_inc(o_copied, 1)

            def copy_ont(i):
                if i >= 2:
                    filled(act, "proj", i - 2)
                filled(act, "on_turn", i)
                ins = act.activation(o_nt[:, i % 2, :], bank_of("on_turn", i)[:, 0:T], ACT.Copy)
                ins.then_inc(ont_ready, 1)

            def hidden_gelu(half, i):
                step = f"hidden{half}"
                if i >= 2 and half == 0:
                    filled(act, "down", i - 2)
                filled(act, step, i)
                for k in range(2):
                    c = 2 * half + k
                    ins = act.activation(hidden[:, i % 2, c, :], bank_of(step, i)[:, k * T:(k + 1) * T],
                                         ACT.Gelu, bias=col("L0_cond_b1", c))
                ins.then_inc(hidden_ready, 1)

            def gate_gelu(half, i):
                step = f"gate{half}"
                if 2 * (i - B) + half >= 2:
                    act.wait_ge(hidden_ready, 2 * i + half - 1)
                filled(act, step, i)
                act.activation(gelu[:, half, :, :], bank_of(step, i)[:].rearrange("f (k t) -> f k t", k=2),
                               ACT.Gelu).then_inc(gelu_ready, 1)

            for _, step, i, n in PROGRAMS["scalar"]:
                if step == "exp":
                    exponentials(i, n, prob_units(i)[n])
                elif step == "copy_o":
                    copy_o(i, n)
                elif step == "rows":
                    act.wait_ge(cols_ready, 1)
                    act.activation(silu[:, 0, :], cols[:, 0:B], ACT.Exp, scale=-1.0).then_inc(neg_exp, 1)
                elif step == "gelu_table":
                    act.wait_ge(minus_half_ready, 1)
                    act.activation(unused[:], minus_half[:], ACT.Gelu)
                elif step == "times":
                    act.wait_ge(tz_ready, 1)
                    act.activation(tsilu[:, 1, :, :], tsilu[:, 0, :, :], ACT.Exp, scale=-1.0).then_inc(texp_ready, 1)
                elif step in ("affine1", "affine2"):
                    affine(int(step[-1]) - 1, i)
                elif step == "high":
                    high_part(i) if i < B else high_part1(i)
                elif step == "copy_v":
                    copy_v(i)
                elif step in ("move_max0", "move_max1"):
                    move_max(i, int(step[-1]))
                elif step == "copy_on":
                    copy_ont(i)
                elif step in ("gelu0", "gelu1"):
                    gelu_half = int(step[-1])
                    hidden_gelu(gelu_half, i) if i < B else gate_gelu(gelu_half, i)

        @block.vector
        def _(dve):
            links = [0]

            def link(ins):
                links[0] += 1
                ins.then_inc(vchain, 1)
                dve.wait_ge(vchain, links[0])

            def cond_silu():
                filled(dve, "rows", 0)
                dve.tensor_copy(cols[:], bank_of("rows", 0)[:, 0:NROWS]).then_inc(cols_ready, 1)
                dve.wait_ge(neg_exp, 1)
                link(dve.tensor_scalar_add(silu[:, 1, :], silu[:, 0, :], 1.0))
                link(dve.reciprocal(silu[:, 2, :], silu[:, 1, :]))
                dve.tensor_tensor(silu[:, 3, :], silu[:, 2, :], cols[:, 0:B], ALU.mult).then_inc(silu_ready, 1)
                dve.wait_ge(silu_ready, 1)
                dve.tensor_copy(silu_wide[:], silu[:, 3, :].unsqueeze(2).to_broadcast([P, B, P])).then_inc(wide_ready, 1)

            def norm_mods():
                filled(dve, "mods", 0)
                for n, chunk in enumerate((0, 1, 3, 4)):
                    ins = dve.tensor_scalar(mod[:, n, :], bank_of("mods", 0)[:, n * B:(n + 1) * B],
                                            col("L0_cond_bada", chunk), float(n % 2), ALU.add, ALU.add)
                link(ins)
                for w in range(2):
                    dve.tensor_scalar(mul_c[:, 0, w, :], mod[:, 2 * w + 1, :], col(f"L0_cond_g{w + 1}"), None, ALU.mult)
                    ins = dve.scalar_tensor_tensor(add_c[:, 0, w, :], mod[:, 2 * w + 1, :], col(f"L0_cond_be{w + 1}"),
                                                   mod[:, 2 * w, :], ALU.mult, ALU.add)
                ins.then_inc(norm0_ready, 1)

            def gate_rows(k):
                step = f"gates{k}"
                if k == 0:
                    dve.wait_ge(wide_loaded, 16)
                filled(dve, step, 0)
                dve.tensor_tensor(gates[:, k, :, :], bank_of(step, 0)[:].rearrange("p (b d) -> p b d", b=B),
                                  wide[:, k, :].unsqueeze(1).to_broadcast([P, B, D]), ALU.add).then_inc(gates_ready, 1)

            def times():
                filled(dve, "times", 0)
                bank = bank_of("times", 0)
                for k in range(2):
                    ins = dve.tensor_scalar(tsilu[:, 0, k, :], bank[:, k * B:(k + 1) * B], col(f"L1_cond_t{k + 1}_b1"),
                                            None, ALU.add)
                ins.then_inc(tz_ready, 1)
                dve.wait_ge(texp_ready, 1)
                link(dve.tensor_scalar_add(tsilu[:, 2, :, :], tsilu[:, 1, :, :], 1.0))
                link(dve.reciprocal(tsilu[:, 3, :, :], tsilu[:, 2, :, :]))
                dve.tensor_tensor(tsilu[:, 4, :, :], tsilu[:, 3, :, :], tsilu[:, 0, :, :], ALU.mult).then_inc(tsilu_ready, 1)

            def times2():
                filled(dve, "times2", 0)
                bank = bank_of("times2", 0)
                for k in range(2):
                    ins = dve.tensor_scalar(tmod[:, k, 0, :], bank[:, 2 * k * B:(2 * k + 1) * B],
                                            col(f"L1_cond_t{k + 1}_b2", 0), 1.0, ALU.add, ALU.add)
                    dve.tensor_scalar(add_c[:, 1, k, :], bank[:, (2 * k + 1) * B:(2 * k + 2) * B],
                                      col(f"L1_cond_t{k + 1}_b2", 1), None, ALU.add)
                link(ins)
                for k in range(2):
                    ins = dve.tensor_scalar(mul_c[:, 1, k, :], tmod[:, k, 0, :], col(f"L1_cond_w_norm{k + 1}"),
                                            None, ALU.mult)
                ins.then_inc(norm1_ready, 1)

            def stats(w, i):
                layer, b = divmod(i, B)
                if w == 0:
                    if layer == 0:
                        dve.wait_ge(x_loaded[b], 16)
                    else:
                        dve.wait_ge(end_ready, i - B + 1)
                else:
                    dve.wait_ge(mid_ready, i + 1)
                if i >= 2:
                    dve.wait_ge(rstd_ready[w], i - 1)
                x = xs[2 * layer + w]
                for j in range(NT):
                    ins = dve.bn_stats(bn[:, w, j, :], x[:, b * NT + j, :])
                link(ins)
                mv = mean_var[:, w, i % 2]
                for j in range(NT):
                    ins = dve.bn_aggr(mv[:, j, :], bn[:, w, j, :])
                link(ins)
                if layer:
                    link(dve.tensor_tensor(square[:], mv[:, :, 0], mv[:, :, 0], ALU.mult))
                    ins = dve.scalar_tensor_tensor(var_eps[:, w, i % 2, :], square[:], EPS, mv[:, :, 1], ALU.add, ALU.add)
                else:
                    ins = dve.tensor_scalar_add(var_eps[:, w, i % 2, :], mv[:, :, 1], EPS)
                ins.then_inc(stats_ready[w], 1)

            def centre(w, i):
                layer, b = divmod(i, B)
                x = xs[2 * layer + w]
                if i >= 2:
                    filled(dve, f"turn{w + 1}", i - 2)
                dve.wait_ge(rstd_ready[w], i + 1)
                for j in range(NT):
                    scale = rstd[:, w, i % 2, j:j + 1]
                    if layer == 0:
                        ins = dve.tensor_scalar(xn[w][:, i % 2, j, :], x[:, b * NT + j, :],
                                                mean_var[:, w, i % 2, j, 0:1], scale, ALU.subtract, ALU.mult)
                    else:
                        ins = dve.tensor_scalar(xn[w][:, i % 2, j, :], x[:, b * NT + j, :], scale, None, ALU.mult)
                    ins.then_inc(xn_ready[w], 1)

            def split(step, i):
                high, middle, low = (parts[:, i % 2, n:n + 4:3, :] for n in range(3))
                if step == "split":
                    full = bank_of("qk", i)[:].rearrange("c (k t) -> c k t", k=2) if i < B else qk_full[:]
                    dve.wait_ge(high_ready, i + 1)
                    dve.tensor_tensor(rest[:], full, high, ALU.subtract).then_inc(rest_ready, 1)
                elif step == "middle":
                    dve.wait_ge(rest_ready, i + 1)
                    dve.tensor_copy(middle, rest[:]).then_inc(middle_ready, 1)
                else:
                    dve.wait_ge(middle_ready, i + 1)
                    dve.tensor_tensor(low, rest[:], middle, ALU.subtract).then_inc(low_ready, 1)

            def rotate(i, sines):
                step = "qk_rot" if sines else "qk"
                filled(dve, step, i)
                dst = rot_b if sines else rot_a
                for k in range(2):
                    ins = dve.scalar_tensor_tensor(dst[:, k, :], bank_of(step, i)[:, k * T:(k + 1) * T],
                                                   col("rotated bq" if sines else "turned bq", k), rope[:, int(sines), :], ALU.add, ALU.mult)
                ins.then_inc(rot_ready, 1)
                if sines:
                    dve.wait_ge(rot_ready, 2 * (i - B + 1))
                    dve.tensor_tensor(qk_full[:], rot_a[:], rot_b[:], ALU.add).then_inc(full_ready, 1)

            def add_bv(i):
                b = i % B
                dve.wait_ge(pv_done, pv_number(i - B, 3, 1) + 1)
                if i == B:
                    dve.wait_ge(wide_loaded, 16)
                filled(dve, "v", i)
                ins = dve.tensor_tensor(v_sb[:, b * NT:(b + 1) * NT, :, 0:HD],
                                        bank_of("v", i)[:, 0:T].rearrange("k (j h d) -> k j h d", j=NT, h=H),
                                        bv_row.rearrange("k (h d) -> k h d", h=H).unsqueeze(1)
                                        .to_broadcast([P, NT, H, HD]), ALU.add)
                ins.then_inc(v_ready, 1)

            def maxima(i, n, unit):
                qb, p, s0, heads, keys = unit
                number = s_number(i, n)
                if n == 0 and i >= 2:
                    dve.wait_ge(max_split, 2 * (i - 1))
                dve.wait_ge(s_filled, number + 1)
                dve.tensor_reduce(row_max[:, i % 2, s0 // MS, qb, p, s0 % MS:s0 % MS + heads],
                                  s_bank[number % S_BANKS][:].rearrange("q (s k) -> q s k", s=heads), AX_X, ALU.max)\
                   .then_inc(max_done, 1)

            def normalise(i, qb):
                step = f"out_turn{qb}"
                filled(dve, step, i)
                if i >= 2 and qb == 0:
                    filled(dve, "on_turn", i - 2)
                o = bank_of(step, i)[:].rearrange("q (h w) -> q h w", h=H)
                link(dve.reciprocal(denom[:, qb, :], o[:, :, HD]))
                ins = dve.tensor_tensor(o_n[:, i % 2, qb, :].rearrange("q (h d) -> q h d", h=H), o[:, :, 0:HD],
                                        denom[:, qb, :].unsqueeze(2).to_broadcast([P, H, HD]), ALU.mult)
                ins.then_inc(on_ready, 1)

            def add_attention(i):
                layer, b = divmod(i, B)
                filled(dve, "proj", i)
                dve.wait_ge(x_bias_ready[0], i + 1)
                dve.tensor_tensor(xs[2 * layer + 1][:, b * NT:(b + 1) * NT, :],
                                  bank_of("proj", i)[:, 0:T].rearrange("t (j d) -> t j d", j=NT),
                                  x_bias[0][:, i % 2, :, :], ALU.add).then_inc(mid_ready, 1)

            def times_up(half, i):
                step = f"up{half}"
                if half == 0:
                    filled(dve, "down", i - 2)
                filled(dve, step, i)
                dve.wait_ge(gelu_ready, 2 * (i - B) + half + 1)
                dve.tensor_tensor(hidden[:, i % 2, 2 * half:2 * half + 2, :],
                                  bank_of(step, i)[:].rearrange("f (k t) -> f k t", k=2), gelu[:, half, :, :],
                                  ALU.mult).then_inc(hidden_ready, 1)

            def add_mlp_out(i):
                layer, b = divmod(i, B)
                filled(dve, "down", i)
                if layer == 0:
                    dve.wait_ge(x_bias_ready[1], i + 1)
                old = xs[3][:, b * NT:(b + 1) * NT, :] if layer else x_bias[1][:, i % 2, :, :]
                dve.tensor_tensor(xs[2 * layer + 2][:, b * NT:(b + 1) * NT, :],
                                  bank_of("down", i)[:, 0:T].rearrange("t (j d) -> t j d", j=NT),
                                  old, ALU.add).then_inc(end_ready, 1)

            for _, step, i, n in PROGRAMS["vector"]:
                if step == "maxima":
                    maxima(i, n, score_units(i)[n])
                elif step == "rows":
                    cond_silu()
                elif step == "mods":
                    norm_mods()
                elif step in ("gates0", "gates1"):
                    gate_rows(int(step[-1]))
                elif step == "times":
                    times()
                elif step == "times2":
                    times2()
                elif step in ("stats1", "stats2"):
                    stats(int(step[-1]) - 1, i)
                elif step in ("centre1", "centre2"):
                    centre(int(step[-1]) - 1, i)
                elif step in ("rotate0", "rotate1"):
                    rotate(i, step == "rotate1")
                elif step in ("split", "middle", "low"):
                    split(step, i)
                elif step == "add_bv":
                    add_bv(i)
                elif step in ("normalise0", "normalise1"):
                    normalise(i, int(step[-1]))
                elif step == "add_attention":
                    add_attention(i)
                elif step in ("times_up0", "times_up1"):
                    times_up(int(step[-1]), i)
                elif step == "add_mlp":
                    add_mlp_out(i)

        @block.gpsimd
        def _(pool):
            links = [0]

            def link(ins):
                links[0] += 1
                ins.then_inc(pchain, 1)
                pool.wait_ge(pchain, links[0])

            def setup0():
                pool.memset(minus_half[:], -0.5).then_inc(minus_half_ready, 1)
                pool.wait_ge(minus_half_ready, 1)
                pool.memset(stacks[:, 0, :, 1, :].bitcast(F32), minus_one_pair).then_inc(minus_ones, 1)
                pool.wait_ge(loaded["ident"], 16)
                pool.tensor_copy(ident_bf[:], ident).then_inc(casts_ready, 1)

            def cast_mask():
                pool.wait_ge(loaded["layer0"], 16)
                pool.tensor_copy(mask_bf[:], mask).then_inc(casts_ready, 1)

            def setup_b(b):
                if b:
                    pool.memset(stacks[:, b, :, 1, :].bitcast(F32), minus_one_pair).then_inc(minus_ones, 1)
                link(pool.memset(v_sb[:, b * NT:(b + 1) * NT, :, :], 0.0))
                pool.memset(v_sb[:, b * NT:(b + 1) * NT, :, HD:HD + 1], 1.0).then_inc(v_ones, 1)

            def setup_gated():
                pool.wait_ge(gates_ready, 2)
                pool.wait_ge(wide_loaded, 16)
                pool.tensor_tensor(w_projg[:], gates[:, 0, :, :], w_proj.unsqueeze(1).to_broadcast([P, B, D]), ALU.mult)
                link(pool.tensor_tensor(add_attn[:], gates[:, 0, :, :], bproj_row.unsqueeze(1).to_broadcast([P, B, D]),
                                        ALU.mult))
                ins = pool.tensor_tensor(add_mlp[:], gates[:, 1, :, :], b2_row.unsqueeze(1).to_broadcast([P, B, D]),
                                         ALU.mult)
                ins.then_inc(gated_ready, 1)
                for b in range(B):
                    ins = pool.tensor_tensor(w_2g[:, b, :, :], w_2, gates[:, 1, b, :].unsqueeze(1)
                                             .to_broadcast([P, FC, D]), ALU.mult)
                ins.then_inc(gated_ready, 1)

            def root(w, i):
                if i >= 2:
                    pool.wait_ge(xn_ready[w], NT * (i - 1))
                pool.wait_ge(stats_ready[w], i + 1)
                pool.tensor_tensor(rstd[:, w, i % 2, :], var_eps[:, w, i % 2, :], minus_half[:], ALU.pow)\
                    .then_inc(rstd_ready[w], 1)

            def add_bias(w, i):
                layer, b = divmod(i, B)
                if layer and w:
                    return
                if i >= 2:
                    pool.wait_ge(end_ready if w else mid_ready, i - 1)
                if layer == 0:
                    pool.wait_ge(gated_ready, 1)
                elif w == 0:
                    pool.wait_ge(wide_loaded, 16)
                if w:
                    pool.wait_ge(mid_ready, i + 1)
                elif layer:
                    pool.wait_ge(end_ready, i - B + 1)
                else:
                    pool.wait_ge(x_loaded[b], 16)
                bias = bo_row if layer else (add_mlp if w else add_attn)[:, b, :]
                pool.tensor_tensor(x_bias[w][:, i % 2, :, :], xs[2 * layer + w][:, b * NT:(b + 1) * NT, :],
                                   bias.unsqueeze(1).to_broadcast([P, NT, D]), ALU.add).then_inc(x_bias_ready[w], 1)

            def split_max(i, half):
                buf = i % 2
                pool.wait_ge(max_done, s_number(i, len(score_units(i)) // (2 - half)))
                if i >= 2:
                    filled(pool, f"max_turn{half}", i - 2)
                part = max_parts[:, buf, half].rearrange("q b p n s -> q (b p) n s")
                full, rest1 = (x.rearrange("q b p s -> q (b p) s") for x in (row_max[:, buf, half], max_rest[:, buf, half]))
                link(pool.tensor_copy(part[:, :, 0, :], full))
                link(pool.tensor_tensor(rest1, full, part[:, :, 0, :], ALU.subtract))
                link(pool.tensor_copy(part[:, :, 1, :], rest1))
                pool.tensor_tensor(part[:, :, 2, :], rest1, part[:, :, 1, :], ALU.subtract).then_inc(max_split, 1)

            def mask_probs(i, n, unit):
                gs, kb, parity = unit
                number = t_number(i, n)
                pool.wait_ge(exp_done, number + 1)
                v = probs[:, kb, 4 * gs[0] + parity:4 * gs[-1] + 4:2, kb * P:(kb + 1) * P]
                pool.affine_select(out=v, in_=v, pattern=[[0, 2 * len(gs)], [1, P]], compare_op=ALU.is_ge, fill=0.0,
                    base=0, channel_multiplier=-1).then_inc(masked, 1)

            minus_one_pair = float(np.frombuffer(np.uint32(0xBF80BF80).tobytes(), np.float32)[0])
            for _, step, i, n in PROGRAMS["gpsimd"]:
                if step == "mask_probs":
                    mask_probs(i, n, prob_units(i)[n])
                elif step == "start":
                    setup0()
                elif step == "cast_mask":
                    cast_mask()
                elif step == "gated":
                    setup_gated()
                elif step in ("root1", "root2"):
                    root(int(step[-1]) - 1, i)
                elif step == "set_ones":
                    setup_b(i)
                elif step in ("split_max0", "split_max1"):
                    split_max(i, int(step[-1]))
                elif step in ("add_bias1", "add_bias2"):
                    add_bias(int(step[-1]) - 1, i)


def turned(n):
    return n.reshape(*n.shape[:-1], HALF, 2, HD).swapaxes(-3, -2).swapaxes(-2, -1).reshape(n.shape)


def rotated(n):
    return n.reshape(*n.shape[:-1], H, 2, HD // 2)[..., ::-1, :].reshape(n.shape)


def laid_out(v):
    inv = (1.0 / 10000.0 ** (np.arange(0, HD, 2, dtype=np.float32) / np.float32(HD))).astype(np.float32)
    angle = (np.arange(T, dtype=np.float32)[:, None] * inv[None, :]).astype(np.float32)
    d = (np.arange(P) // HALF) % HD
    sign = np.where(d < HD // 2, np.float32(-1), np.float32(1))
    cos, sin = (f(angle).astype(np.float32)[:, d % (HD // 2)].T for f in (np.cos, np.sin))
    ahead = np.arange(P)[None, :] > np.arange(P)[:, None]
    chunks = lambda w: w.reshape(FC, P, D).transpose(1, 0, 2).reshape(P, FC * D)
    qkv = v["L0_cond_Wqkv"]
    bq, bk = v["L1_cond_bq"], v["L1_cond_bk"]
    vectors = {"turned bq": turned(bq), "turned bk": turned(bk),
               "rotated bq": turned(rotated(bq)), "rotated bk": turned(rotated(bk))}
    bada = v["L0_cond_bada"]
    rows = [vectors[name] if name in vectors else v[name] for name, _ in ROWS]
    return {
        "x": v["x"],
        "rows": np.concatenate([r.reshape(-1, D) for r in rows]),
        "wide": np.concatenate([bada[2 * D:3 * D], bada[5 * D:], *(v[name] for name in WIDE[2:])]),
        "ident": np.eye(P, dtype=np.float32),
        "early": np.concatenate([turned(qkv[:, :D]), turned(qkv[:, D:2 * D]), qkv[:, 2 * D:]], axis=1),
        "ada": v["L0_cond_Wada"],
        "layer0": np.concatenate([np.where(ahead, np.float32(MASKED), np.float32(0)), v["L0_cond_Wproj"],
                                  v["L0_cond_W1"], chunks(v["L0_cond_W2"])], axis=1),
        "attn1": np.concatenate([cos, sin * sign[:, None], turned(v["L1_cond_wq"]), turned(v["L1_cond_wk"]),
                                 turned(rotated(v["L1_cond_wq"])), turned(rotated(v["L1_cond_wk"])),
                                 v["L1_cond_t1_w1"], v["L1_cond_t2_w1"], v["L1_cond_t1_w2"], v["L1_cond_t2_w2"],
                                 v["L1_cond_wv"], v["L1_cond_wo"]], axis=1),
        "mlp1": np.concatenate([v["L1_cond_w_gate"], v["L1_cond_w_up"], chunks(v["L1_cond_w_down"])], axis=1),
    }


def kernel(**inputs):
    import concourse.bacc as _bacc
    from concourse.bass_utils import run_bass_kernel_spmd as _run

    nc = _bacc.Bacc("TRN2", target_bir_lowering=False, num_devices=1)
    arrays, a = {}, {}
    for name, value in laid_out({k: np.asarray(v) for k, v in inputs.items()}).items():
        v = np.ascontiguousarray(value)
        arrays[f"in_{name}"] = v
        a[name] = nc.dram_tensor(f"in_{name}", v.shape, mybir.dt.from_np(v.dtype), kind="ExternalInput").ap()
    out = nc.dram_tensor("out_0", (B, T, D), F32, kind="ExternalOutput").ap()
    build(nc, a, out)
    r = _run(nc, [arrays], core_ids=[0])
    return r.results[0]["out_0"]
```
